# Optimizing a Trainium2 kernel written in Bass

```python
import numpy as np
import jax
import jax.numpy as jnp

def _softmax(x, axis=-1):
    return jax.nn.softmax(x, axis=axis)

def _gelu(x):
    return jax.nn.gelu(x, approximate=True)

def _silu(x):
    return jax.nn.silu(x)

def _sigmoid(x):
    return jax.nn.sigmoid(x)

def _layernorm(x, axis=-1, eps=1e-05):
    m = jnp.mean(x, axis=axis, keepdims=True)
    v = jnp.var(x, axis=axis, keepdims=True)
    return (x - m) / jnp.sqrt(v + eps)

def _scatter_add(tgt, idx, src, axis=0):
    return tgt.at[idx].add(src)

def _segment_sum(src, seg, n):
    return jax.ops.segment_sum(src, seg, n)
kernel_name = 'mk_adj_ffn_d1_adj_r2_d27da9'

def setup_inputs(seed: int=0):
    np.random.seed(seed)
    _w = jnp.asarray

    def _rec_inputs():
        import jax
        import jax.numpy as jnp
        _gk = jax.random.key(seed)
        x = -0.0001117 + 0.9999 * jax.random.normal(jax.random.fold_in(_gk, 1), (64, 128, 256), jnp.float32)
        _a = jax.random.bernoulli(jax.random.fold_in(_gk, 2), 0.0625, (128, 128))
        _a = jnp.logical_or(_a, jnp.swapaxes(_a, -1, -2))
        _a = jnp.logical_or(_a, jnp.eye(128, dtype=bool))
        adj = _a.astype(jnp.int32)
        return (x, adj)
    x, adj = _rec_inputs()

    def _L0_gnn_setup():
        import jax, jax.numpy as jnp
        import numpy as np
        B, N, F, F1 = (512, 75, 256, 128)
        NEG = -1000000000.0
        ALPHA = 0.2
        key = jax.random.key(seed)
        k1, k2, k3, k4 = jax.random.split(key, 4)
        X = jax.random.normal(k1, (B, N, F), dtype=jnp.float32)
        A = jax.random.randint(k2, (N, N), 0, 2, dtype=jnp.int32)
        W = jax.random.normal(k3, (F, F1), dtype=jnp.float32) * (1.0 / np.sqrt(F))
        a = jax.random.normal(k4, (2, F1, 1), dtype=jnp.float32) * (1.0 / np.sqrt(F1))
        return {'X': X, 'A': A, 'W': W, 'a': a}
    _L0_gnn_all = _L0_gnn_setup()
    _L0_gnn_in = {k: v for k, v in _L0_gnn_all.items() if k in ('W', 'a')}
    del _L0_gnn_all

    def _L0_ffn_setup():
        import jax, jax.numpy as jnp
        import numpy as np
        D_MODEL = 256
        D_FF = 256
        N_EXPERTS = 16
        TOP_K = 3
        BATCH, SEQ = (1, 1024)

        def _swiglu(combined):
            gate, up = jnp.split(combined, 2, axis=-1)
            return jax.nn.silu(gate) * up
        key = jax.random.key(seed)
        ks = jax.random.split(key, 6)
        x = jax.random.normal(ks[0], (BATCH, SEQ, D_MODEL), dtype=jnp.float32)
        gate_w = 0.01 * jax.random.normal(ks[1], (N_EXPERTS, D_MODEL), dtype=jnp.float32)
        expert_bias = jnp.zeros((N_EXPERTS,), dtype=jnp.float32)
        shared_gate_up = 0.02 * jax.random.normal(ks[2], (2 * D_FF, D_MODEL), dtype=jnp.float32)
        shared_down = 0.02 * jax.random.normal(ks[3], (D_MODEL, D_FF), dtype=jnp.float32)
        expert_gate_up = 0.02 * jax.random.normal(ks[4], (N_EXPERTS, 2 * D_FF, D_MODEL), dtype=jnp.float32)
        expert_down = 0.02 * jax.random.normal(ks[5], (N_EXPERTS, D_MODEL, D_FF), dtype=jnp.float32)
        return {'x': x, 'gate_w': gate_w, 'expert_bias': expert_bias, 'shared_gate_up': shared_gate_up, 'shared_down': shared_down, 'expert_gate_up': expert_gate_up, 'expert_down': expert_down}
    _L0_ffn_all = _L0_ffn_setup()
    _L0_ffn_in = {k: v for k, v in _L0_ffn_all.items() if k in ('gate_w', 'expert_bias', 'shared_gate_up', 'shared_down', 'expert_gate_up', 'expert_down')}
    del _L0_ffn_all
    return {'x': x, 'adj': adj, 'L0_gnn_W': _L0_gnn_in['W'], 'L0_gnn_a': _L0_gnn_in['a'], 'L0_ffn_gate_w': _L0_ffn_in['gate_w'], 'L0_ffn_expert_bias': _L0_ffn_in['expert_bias'], 'L0_ffn_shared_gate_up': _L0_ffn_in['shared_gate_up'], 'L0_ffn_shared_down': _L0_ffn_in['shared_down'], 'L0_ffn_expert_gate_up': _L0_ffn_in['expert_gate_up'], 'L0_ffn_expert_down': _L0_ffn_in['expert_down']}

def reference(x, adj, L0_gnn_W, L0_gnn_a, L0_ffn_gate_w, L0_ffn_expert_bias, L0_ffn_shared_gate_up, L0_ffn_shared_down, L0_ffn_expert_gate_up, L0_ffn_expert_down):
    import jax
    import jax.numpy as jnp

    def _L0_gnn_ref(X, A, W, a):
        import jax, jax.numpy as jnp
        import numpy as np
        B, N, F, F1 = (512, 75, 256, 128)
        NEG = -1000000000.0
        ALPHA = 0.2
        h = jnp.einsum('bnf,fo->bno', X, W)
        att_self = jnp.einsum('bno,od->bnd', h, a[0])
        att_neigh = jnp.einsum('bno,od->bnd', h, a[1])
        e = att_self + jnp.swapaxes(att_neigh, 1, 2)
        e = jax.nn.leaky_relu(e, ALPHA)
        adj = A.astype(h.dtype)
        e = e + NEG * (1.0 - adj)[None, :, :]
        alpha = jax.nn.softmax(e, axis=-1)
        out = jnp.einsum('bij,bjo->bio', alpha, h)
        return jnp.concatenate([out, h], axis=-1)

    def _L0_ffn_ref(x, gate_w, expert_bias, shared_gate_up, shared_down, expert_gate_up, expert_down):
        import jax, jax.numpy as jnp
        import numpy as np
        D_MODEL = 256
        D_FF = 256
        N_EXPERTS = 16
        TOP_K = 3
        BATCH, SEQ = (1, 1024)

        def _swiglu(combined):
            gate, up = jnp.split(combined, 2, axis=-1)
            return jax.nn.silu(gate) * up
        B, S, D = x.shape
        xf = x.reshape(-1, D)
        shared_out = _swiglu(xf @ shared_gate_up.T) @ shared_down.T
        logits = xf @ gate_w.T
        affinity = jax.nn.sigmoid(logits)
        routing_scores = affinity + expert_bias
        _, sel = jax.lax.top_k(routing_scores, TOP_K)
        sel_aff = jnp.take_along_axis(affinity, sel, axis=1)
        gating = sel_aff / (sel_aff.sum(axis=-1, keepdims=True) + 1e-09)
        combined = jnp.einsum('td,efd->tef', xf, expert_gate_up)
        hidden = _swiglu(combined)
        expert_out = jnp.einsum('tef,edf->ted', hidden, expert_down)
        sel_out = jnp.take_along_axis(expert_out, sel[:, :, None], axis=1)
        routed_out = jnp.einsum('tk,tkd->td', gating, sel_out)
        out = shared_out + routed_out
        return out.reshape(B, S, D)
    x = x + _L0_gnn_ref(_layernorm(x, axis=-1), adj, L0_gnn_W, L0_gnn_a)
    x = x + _L0_ffn_ref(_layernorm(x, axis=-1), L0_ffn_gate_w, L0_ffn_expert_bias, L0_ffn_shared_gate_up, L0_ffn_shared_down, L0_ffn_expert_gate_up, L0_ffn_expert_down)
    return x

_drawn_inputs = setup_inputs


def setup_inputs(seed=0):
    import zlib

    import numpy as np

    out = dict(_drawn_inputs(seed))
    spreads = {'L0_ffn_expert_bias': (0.0, 0.8)}
    factors = {'L0_ffn_gate_w': 8.0,
     'L0_ffn_shared_gate_up': 4.094,
     'L0_ffn_shared_down': 3.99,
     'L0_ffn_expert_gate_up': 7.222,
     'L0_ffn_expert_down': 7.233}
    for name, (base, spread) in spreads.items():
        noise = np.random.default_rng([zlib.crc32(name.encode()), seed]).standard_normal(out[name].shape)
        drawn = base * np.exp(spread * noise) if base else spread * noise
        out[name] = jnp.asarray(drawn.astype(out[name].dtype))
    for name, factor in factors.items():
        out[name] = (out[name] * factor).astype(out[name].dtype)
    return out
```

```python
from contextlib import ExitStack

import concourse.bass as bass
from concourse import mybir

ALU = mybir.AluOpType
ACT = mybir.ActivationFunctionType
AX_X = mybir.AxisListType.X
F32 = mybir.dt.float32
F32R = mybir.dt.float32r
BF16 = mybir.dt.bfloat16
I32 = mybir.dt.int32
U32 = mybir.dt.uint32

P = 128
TILES = 64
TOKENS = TILES * P
D = 256
KD = D // P
O = 128
FF = 256
KF = FF // P
E = 16
TOP = 3
EPS = 1e-5
SLOPE = 0.2
NEG = -1e9

GS = 4
GROUPS = TILES // GS

REGION = TOKENS + P
TAG, GATE = D, D + E
ROW = D + 2 * E
LIST_ROWS = E * REGION + P
NO_ROW = 4 * TOKENS * TOP

SLOTS = (TOKENS * TOP + E * (P - 1)) // P
SLOTS += -SLOTS % 4
WIDE = 2 * FF
WX = KD * WIDE + KF * D
RING = 4

C_ID, C_LOW = 0, P
C_IOTA = 2 * P
C_BASE = C_IOTA + E
C_TAG = C_BASE + E
C_TILE = C_TAG + GS
C_PAD = C_TILE + 2
C_ONE = C_PAD + ROW
C_ALL = C_ONE + E

LN1_STEPS, ATT_STEPS, X1_STEPS, ROUTE_STEPS, POS_STEPS = 7, 4, 10, 13, 4
GROUP_SCATTERS = GS * TOP


def constants():
    import numpy as np

    c = np.zeros((P, C_ALL), np.float32)
    p = np.arange(P)
    c[:, C_ID:C_ID + P] = np.eye(P)
    c[:, C_LOW:C_LOW + P] = p[:, None] < p[None, :]
    c[:, C_IOTA:C_IOTA + E] = np.arange(E)
    c[:, C_BASE:C_BASE + E] = np.arange(E) * REGION
    c[:, C_TAG:C_TAG + GS] = TOP * (P * np.arange(GS)[None, :] + p[:, None]) - 1
    c[:, C_TILE:C_TILE + 2] = P * np.arange(2)[None, :] + p[:, None]
    c[:, C_PAD + TAG:C_PAD + GATE] = NO_ROW
    c[:, C_ONE:C_ONE + E] = 1.0
    return c


def build(nc, x, adj, w, wt, at, gate_wt, bias, weights, consts, out):
    with ExitStack() as ctx:
        def sb(name, shape, dt):
            return ctx.enter_context(nc.sbuf_tensor(name, shape, dt))

        def sem(name):
            return ctx.enter_context(nc.semaphore(name))

        def wait(eng, s, value):
            if not (isinstance(value, int) and value <= 0):
                eng.wait_ge(s, value)

        def wait_alone(eng, s, value):
            value = value if isinstance(value, int) else eng.to_reg(value)
            eng.wait_ge(s_const, 16 * CONSTS)
            eng.wait_ge(s, value)

        lists = nc.dram_tensor("lists", [LIST_ROWS, ROW], F32).ap()
        split_w = nc.dram_tensor("split_w", [E, P, 2, WX], F32).ap()
        routed = nc.dram_tensor("routed", [TOKENS * TOP, D], F32).ap()
        routed_t = routed.rearrange("(t p k) d -> t p (k d)", p=P, k=TOP)

        X1 = sb("X1", [P, TILES, D], F32)
        ln2 = sb("ln2", [P, TILES, 2], F32)
        cs = sb("cs", [P, C_ALL], F32)
        ident = cs[:, C_ID:C_ID + P]
        ring = sb("ring", [P, RING, 2, WX], F32R)
        shared = sb("shared", [P, 2, WX], F32R)
        table = sb("table", [1, 3, 2 * P], I32)
        counts_i = sb("counts_i", [1, E], I32)

        wext = sb("wext", [P, KD, O + 2], F32)
        wts = sb("wts", [P, D], F32)
        ats = sb("ats", [P, 2], F32)
        gws = sb("gws", [P, KD, E], F32)
        bias_s = sb("bias_s", [P, E], F32)
        adj_i = sb("adj_i", [P, P], I32)
        mask = sb("mask", [P, P], F32)
        low_ones = sb("low_ones", [P, 2 * P], BF16)
        lower, ones = low_ones[:, 0:P], low_ones[:, P:2 * P]
        wst = sb("wst", [P, WX], F32)
        st = sb("st", [P, GS, 6], F32)
        mv = sb("mv", [P, GS, 2], F32)
        nw1 = sb("nw1", [P, 5, GS], F32)
        ln1 = sb("ln1", [P, 2, GS, 2], F32)
        st2 = sb("st2", [P, GS, 6], F32)
        mv2 = sb("mv2", [P, GS, 2], F32)
        nw2 = sb("nw2", [P, 5, GS], F32)
        xn1 = sb("xn1", [P, 2, GS, D], F32)
        xnT = sb("xnT", [P, KD, GS * P], F32)
        hsb = sb("hsb", [P, 2, GS, O + 2], F32)
        att = sb("att", [P, GS, P], F32)
        nmax = sb("nmax", [P, GS], F32)
        prob = sb("prob", [P, GS, P], F32)
        psums = sb("psums", [P, GS], F32)
        rsum = sb("rsum", [P, GS], F32)
        probT = sb("probT", [P, GS, P], F32)
        x2 = [sb(f"x2_{i}", [P, GS, ROW], F32) for i in range(2)]
        x2T = sb("x2T", [P, KD, GS * P], F32)
        tagbase = sb("tagbase", [P, GS], F32)
        ez = sb("ez", [P, GS, E], F32)
        aff1 = sb("aff1", [P, GS, E], F32)
        aff = sb("aff", [P, GS, E], F32)
        score = sb("score", [P, GS, E], F32)
        top8 = sb("top8", [P, GS, 8], F32)
        topi = sb("topi", [P, GS, 8], U32)
        topf = sb("topf", [P, GS, TOP], F32)
        onehot = sb("onehot", [P, GS, TOP, E], F32)
        taken = sb("taken", [P, GS, E], BF16)
        tag1 = sb("tag1", [P, GS, E], F32)
        tag2 = sb("tag2", [P, GS, E], F32)
        sel = sb("sel", [P, GS, E], F32)
        den = sb("den", [P, 3, GS], F32)
        before = sb("before", [P, 2, E], BF16)
        newly = sb("newly", [P, E], F32)
        rankb = sb("rankb", [P, GS, E], F32)
        selpos = sb("selpos", [P, GS, TOP, E], F32)
        posf = sb("posf", [P, GS, TOP], F32)
        pos = [sb(f"pos_{i}", [P, GS * TOP], I32) for i in range(2)]

        cnt = sb("cnt", [P, E], F32)
        nti = sb("nti", [P, E], I32)
        ntf = sb("ntf", [P, E], F32)
        cum = sb("cum", [P, E], F32)
        ended = sb("ended", [P, 2, E], F32)
        tmp2 = sb("tmp2", [P, 2, E], F32)
        ej = sb("ej", [P, 8, 2], F32)
        tv = sb("tv", [P, 3, 2], F32)

        xs = [sb(f"xs_{i}", [P, ROW], F32) for i in range(4)]
        gate_j = [sb(f"gate_j_{i}", [P, 1], F32) for i in range(4)]
        dest = [sb(f"dest_{i}", [P, 1], I32) for i in range(4)]
        xTh = sb("xTh", [P, 2, KD, P], F32R)
        xTl = sb("xTl", [P, 2, KD, P], F32R)
        gate = sb("gate", [P, 2, FF], F32)
        hid = sb("hid", [P, 2, FF], F32)
        hTh = sb("hTh", [P, 2, KF, P], F32R)
        hTl = sb("hTl", [P, 2, KF, P], F32R)
        ysb = [sb(f"ysb_{i}", [P, D], F32) for i in range(4)]
        yr = ring[:, 0].rearrange("p h c -> p (h c)").bitcast(F32).rearrange("p (u c) -> p u c", u=4)

        bank = [ctx.enter_context(nc.psum_tensor(f"bank{i}", [P, 512], F32)) for i in range(8)]
        p_t = bank[0:2]
        p_h = bank[2:4]
        p_n, p_pt, p_o = bank[4], bank[5], bank[6]
        p_lg = bank[7][:, 0:GS * E]
        p_rk = bank[7][:, 256:256 + GS * E]
        p_xT, p_gu, p_hT, p_y = bank[0:2], bank[2:4], bank[4:6], bank[6:8]

        s_const = sem("const_loaded")
        s_x = [sem(f"x_loaded{i}") for i in range(2)]
        s_wa = sem("wa_product")
        s_prep = sem("vector_prepared")
        s_win = sem("weights_in")
        s_whi = sem("weights_high")
        s_wlo = sem("weights_low")
        s_wout = [sem(f"weights_out{i}") for i in range(2)]
        s_ln1 = sem("ln1_steps")
        s_ex1 = sem("guess1_steps")
        s_ex2 = sem("guess2_steps")
        s_xn1 = sem("xn1_ready")
        s_t1 = sem("xn1_transposed")
        s_xnT = sem("xnT_ready")
        s_h = sem("h_product")
        s_hsb = sem("h_ready")
        s_nb = sem("neighbour_rows")
        s_att = sem("attention_steps")
        s_exp = sem("prob_ready")
        s_tp = sem("prob_transposed")
        s_pT = sem("probT_ready")
        s_out = sem("attended")
        s_x1 = sem("x1_steps")
        s_t2 = sem("x2_transposed")
        s_x2T = sem("x2T_ready")
        s_lg = sem("logits")
        s_ez = sem("exp_logits")
        s_rt = sem("route_steps")
        s_rk = sem("ranks")
        s_pos = sem("position_steps")
        s_scat = [sem(f"scattered{i}") for i in range(2)]
        s_cnt = sem("counts")
        s_tb = sem("table_steps")
        s_rows = sem("table_rows")
        s_pad = [sem(f"padded{i}") for i in range(2)]
        s_xl = [sem(f"list_tile_loaded{i}") for i in range(4)]
        s_w = sem("expert_weights_loaded")
        s_xsh = sem("shared_tile_ready")
        s_tx = sem("tile_transposed")
        s_xh = sem("tile_high")
        s_xlo = sem("tile_low")
        s_gu = sem("gate_up")
        s_sg = sem("gate_ready")
        s_hid = sem("hidden_ready")
        s_th = sem("hidden_transposed")
        s_hh = sem("hidden_high")
        s_hl = sem("hidden_low")
        s_dn = sem("down")
        s_y = sem("result_ready")
        s_dest = sem("dest_ready")
        s_ys = [sem(f"result_scattered{i}") for i in range(4)]
        s_yl = [sem(f"routed_loaded{i}") for i in range(4)]
        s_acc = sem("routed_added")
        s_fin = sem("tile_finished")
        s_store = sem("stored")

        CONSTS = 7
        xg = x.rearrange("(g j) p d -> g p j d", j=GS)

        def each_group(eng, body):
            for n in range(-3, 3):
                body(n, n % 2, n // 2)
            with eng.Fori(1, (GROUPS - 4) // 2) as i:
                body(2 * i + 1, 1, i)
                body(2 * i + 2, 0, i + 1)
            for n in range(GROUPS - 3, GROUPS):
                body(n, n % 2, n // 2)

        def ahead(n, p, r, lag):
            if isinstance(n, int) and not 0 <= n + lag < GROUPS:
                return None
            return n + lag, (p + lag) % 2, r + (p + lag) // 2

        def stages(eng, *parts):
            def step(n, p, r):
                for lag, part in parts:
                    g = ahead(n, p, r, lag)
                    if g is not None:
                        part(*g)
            each_group(eng, step)

        def each_tile(eng, body):
            total = SLOTS + TILES
            for j in range(0, 4):
                body(j, j % 4, j // 4, True)
            with eng.Fori(1, SLOTS // 4 - 1) as i:
                for u in range(4):
                    body(4 * i + u, u, i, True)
            for j in range(SLOTS - 4, SLOTS + 4):
                body(j, j % 4, j // 4, j < SLOTS)
            with eng.Fori(SLOTS // 4 + 1, total // 4 - 1) as i:
                for u in range(4):
                    body(4 * i + u, u, i, False)
            for j in range(total - 4, total + 1):
                body(j, j % 4, j // 4, False)

        def kind(j, in_b, lag):
            if not isinstance(j, int):
                return "list" if in_b else "shared"
            return "list" if 0 <= j + lag < SLOTS else "shared" if SLOTS <= j + lag < SLOTS + TILES else None

        block = ctx.enter_context(nc.Block())

        @block.sync
        def _(sp):
            for dst, src in ((cs[:], consts), (wts[:], wt), (ats[:], at), (gws[:], gate_wt), (bias_s[:], bias),
                             (adj_i[:], adj), (wext[:, :, 0:O], w)):
                sp.dma_start(dst, src).then_inc(s_const, 16)

            def load_x(c, p, r):
                wait(sp, s_x[p], 16 * r)
                sp.dma_start(X1[:, bass.ds(4 * c, 4), :], xg[bass.ds(c, 1)].squeeze(0)).then_inc(s_x[p], 16)

            def load_weights(m):
                wait(sp, s_wlo, m)
                sp.dma_start(wst[:], weights[bass.ds(m, 1)].squeeze(0)).then_inc(s_win, 16)

            def store_weights(e, p, r):
                sp.wait_ge(s_whi, e + 2)
                sp.wait_ge(s_wlo, e + 2)
                sp.dma_start(split_w[bass.ds(e, 1)].squeeze(0), ring[:, p].bitcast(F32)).then_inc(s_wout[p], 16)

            for c in range(4):
                load_x(c, c % 2, c // 2)
            load_weights(0)
            with sp.Fori(2, GROUPS // 2) as i:
                for p in range(2):
                    load_x(2 * i + p, p, i)

            def expert_weights(n, p, r):
                load_weights(n + 1)
                store_weights(n, p, r)

            stages(sp, (0, expert_weights))

            sp.wait_ge(s_rows, 1)
            pad = cs[:, C_PAD:C_PAD + ROW]
            sp.dma_start(lists[E * REGION:E * REGION + P, :], pad).then_inc(s_pad[0], 16)
            for e in range(0, E, 2):
                c = sp.value_load(counts_i[0:1, e:e + 1], min_val=0, max_val=TOKENS)
                sp.dma_start(lists[bass.ds(c + e * REGION, P), :], pad).then_inc(s_pad[0], 16)
            sp.wait_ge(s_wout[0], 16 * (E // 2))
            sp.wait_ge(s_wout[1], 16 * (E // 2))
            for e in range(RING - 1):
                wait(sp, s_w, 16 * e)
                sp.dma_start(ring[:, e].bitcast(F32), split_w[e]).then_inc(s_w, 16)
            sp.wait_ge(s_scat[0], 16 * GROUP_SCATTERS * (GROUPS // 2))
            sp.wait_ge(s_scat[1], 16 * GROUP_SCATTERS * (GROUPS // 2))
            sp.wait_ge(s_pad[0], 16 * (E // 2 + 1))
            sp.wait_ge(s_pad[1], 16 * (E // 2))

            def load_tile(j, u):
                row = sp.value_load(table[0:1, 1, bass.ds(j, 1)], min_val=0, max_val=E * REGION)
                sp.dma_start(xs[u][:], lists[bass.ds(row, P), :]).then_inc(s_xl[u], 16)

            def next_expert(j):
                first = sp.value_load(table[0:1, 2, bass.ds(j, 1)], min_val=0, max_val=1)
                with sp.If(first == 1):
                    e = sp.value_load(table[0:1, 0, bass.ds(j, 1)], min_val=0, max_val=E - RING)
                    sp.wait_ge(s_dn, j)
                    sp.wait_ge(s_w, 16 * (e + RING - 1))
                    sp.dma_start(ring[:, bass.ds((e + RING - 1) % RING, 1)].squeeze(1).bitcast(F32),
                                 split_w[bass.ds(e + RING - 1, 1)].squeeze(0)).then_inc(s_w, 16)
                with sp.Else():
                    pass

            for j in range(3):
                load_tile(j, j)

            def step_b(j, u, r, in_b):
                ahead = 3
                if kind(j, in_b, ahead) == "list":
                    wait(sp, s_tx, j)
                    wait(sp, s_dest, j)
                    load_tile(j + ahead, (u + ahead) % 4)
                if isinstance(j, int) and j == 0:
                    sp.wait_ge(s_w, 16 * (RING - 1))
                    sp.dma_start(ring[:, RING - 1].bitcast(F32), split_w[RING - 1]).then_inc(s_w, 16)
                elif kind(j, in_b, 0) == "list":
                    next_expert(j)
                if kind(j, in_b, 0) == "shared":
                    if isinstance(j, int) and j == SLOTS:
                        for i in range(4):
                            sp.wait_ge(s_ys[i], 16 * (SLOTS // 4))
                    wait(sp, s_fin, 2 * (j - SLOTS - 3) - 1)
                    sp.dma_start(yr[:, u], routed_t[bass.ds(j - SLOTS, 1)].squeeze(0)).then_inc(s_yl[u], 16)
                if kind(j, in_b, -4) == "shared":
                    sp.wait_ge(s_fin, 2 * (j - SLOTS - 3))
                    sp.dma_start(out[bass.ds(j - SLOTS - 4, 1)].squeeze(0),
                                 X1[:, bass.ds(j - SLOTS - 4, 1)].squeeze(1)).then_inc(s_store, 16)

            each_tile(sp, step_b)
            for t in range(TILES - 3, TILES):
                sp.wait_ge(s_fin, 2 * t + 2)
                sp.dma_start(out[t], X1[:, t]).then_inc(s_store, 16)
            sp.wait_ge(s_store, 16 * TILES)

        @block.gpsimd
        def _(pool):
            def scatter(a, p, r):
                wait_alone(pool, s_pos, POS_STEPS * a + POS_STEPS)
                for j in range(GS):
                    for k in range(TOP):
                        i = TOP * j + k
                        nc.gpsimd.indirect_dma_start(
                            out=lists, out_offset=bass.IndirectOffsetOnAxis(ap=pos[p][:, i:i + 1], axis=0),
                            in_=x2[p][:, j, :], in_offset=None).then_inc(s_scat[p], 16)

            stages(pool, (0, scatter))

            def take_dest(j, u, r):
                wait_alone(pool, s_xl[u], 16 * r + 16)
                wait(pool, s_ys[u], 16 * r)
                e = pool.value_load(table[0:1, 0, bass.ds(j, 1)], min_val=0, max_val=E - 1)
                nc.gpsimd.tensor_copy(dest[u][:], xs[u][:, bass.ds(e + TAG, 1)])
                nc.gpsimd.tensor_copy(gate_j[u][:], xs[u][:, bass.ds(e + GATE, 1)]).then_inc(s_dest, 1)

            def scatter_y(j, u):
                wait_alone(pool, s_y, j + 1)
                pool.wait_ge(s_dest, j + 1)
                nc.gpsimd.indirect_dma_start(
                    out=routed, out_offset=bass.IndirectOffsetOnAxis(ap=dest[u][:, 0:1], axis=0),
                    in_=ysb[u][:], in_offset=None, bounds_check=TOKENS * TOP - 1,
                    oob_is_err=False).then_inc(s_ys[u], 16)

            def add_routed(t, u, r0):
                pool.wait_ge(s_yl[u], 16 * r0 + 16)
                for k in range(1, TOP):
                    if k > 1:
                        pool.wait_ge(s_acc, (TOP - 1) * t + k - 1)
                    nc.gpsimd.tensor_tensor(yr[:, u, 0:D], yr[:, u, 0:D], yr[:, u, k * D:(k + 1) * D],
                                            ALU.add).then_inc(s_acc, 1)

            pool.wait_ge(s_rows, 1)
            for j in range(2):
                take_dest(j, j, 0)

            def step_b(j, u, r, in_b):
                if kind(j, in_b, 2) == "list":
                    take_dest(j + 2, (u + 2) % 4, r + (u + 2) // 4)
                if kind(j, in_b, -1) == "list":
                    scatter_y(j - 1, (u - 1) % 4)
                if kind(j, in_b, 0) == "shared":
                    add_routed(j - SLOTS, u, r - SLOTS // 4)

            each_tile(pool, step_b)

        @block.scalar
        def _(act):
            nc.scalar.preload_act_table_set("natural_log_exp_and_others")
            act.wait_ge(s_const, 16 * CONSTS)

            def split_high(m, p, r):
                act.wait_ge(s_win, 16 * m + 16)
                if isinstance(m, int) and m == 0:
                    nc.scalar.activation(shared[:, 0], wst[:], ACT.Copy).then_inc(s_whi, 1)
                    return
                wait(act, s_wout[p], 16 * r)
                nc.scalar.activation(ring[:, p, 0], wst[:], ACT.Copy).then_inc(s_whi, 1)

            def guess(steps, ln_steps, count, nw, g):
                act.wait_ge(ln_steps, count)
                nc.scalar.activation(nw[:, 1], nw[:, 0], ACT.Ln).then_inc(steps, 1)
                act.wait_ge(steps, 2 * g + 1)
                nc.scalar.activation(nw[:, 2], nw[:, 1], ACT.Exp, scale=-0.5).then_inc(steps, 1)

            def guess1(g, p, r):
                guess(s_ex1, s_ln1, LN1_STEPS * g + 3, nw1, g)

            def guess2(b, p, r):
                guess(s_ex2, s_x1, X1_STEPS * b + 5, nw2, b)

            def exp_logits(a, p, r):
                act.wait_ge(s_lg, a + 1)
                wait(act, s_rt, ROUTE_STEPS * (a - 1) + 1)
                nc.scalar.activation(ez[:].rearrange("p j e -> p (j e)"), p_lg, ACT.Exp, scale=-1.0).then_inc(s_ez, 1)

            def exp_scores(b, p, r):
                act.wait_ge(s_att, ATT_STEPS * b + ATT_STEPS)
                wait(act, s_tp, b)
                for j in range(GS):
                    last = nc.scalar.activation(prob[:, j], att[:, j], ACT.Exp, bias=nmax[:, j:j + 1],
                                                accum_out=psums[:, j:j + 1])
                last.then_inc(s_exp, 1)

            def norm1(c, p, r):
                act.wait_ge(s_ln1, LN1_STEPS * c + LN1_STEPS)
                wait(act, s_t1, c - 1)
                for j in range(GS):
                    last = nc.scalar.activation(xn1[:, p, j], X1[:, bass.ds(4 * c + j, 1)].squeeze(1), ACT.Identity,
                                                bias=ln1[:, p, j, 1:2], scale=ln1[:, p, j, 0:1])
                last.then_inc(s_xn1, 1)

            def copy_probT(b, p, r):
                act.wait_ge(s_tp, b + 1)
                wait(act, s_out, b)
                nc.scalar.activation(probT[:].rearrange("p j e -> p (j e)"), p_pt[:], ACT.Copy).then_inc(s_pT, 1)

            def copy_xnT(c, p, r):
                act.wait_ge(s_t1, c + 1)
                wait(act, s_h, c)
                nc.scalar.activation(xnT[:, 0], p_t[0][:], ACT.Copy)
                nc.scalar.activation(xnT[:, 1], p_t[1][:], ACT.Copy).then_inc(s_xnT, 1)

            def copy_h(c, p, r):
                act.wait_ge(s_h, c + 1)
                wait(act, s_out, c - 1)
                wait(act, s_x1, X1_STEPS * (c - 2) + 2)
                for i in range(2):
                    last = nc.scalar.activation(hsb[:, p, 2 * i:2 * i + 2],
                                                p_h[i][:, 0:2 * (O + 2)].rearrange("p (j n) -> p j n", j=2), ACT.Copy)
                last.then_inc(s_hsb, 1)

            def copy_x2T(b, p, r):
                act.wait_ge(s_t2, b + 1)
                wait(act, s_lg, b)
                nc.scalar.activation(x2T[:, 0], p_t[0][:], ACT.Copy)
                nc.scalar.activation(x2T[:, 1], p_t[1][:], ACT.Copy).then_inc(s_x2T, 1)

            def split_next(n, p, r):
                split_high(n + 1, p, r)

            split_high(0, 0, 0)
            stages(act, (0, copy_x2T), (2, norm1), (0, exp_logits), (1, exp_scores), (2, copy_xnT), (3, guess1),
                   (1, copy_probT), (2, copy_h), (0, split_next), (1, guess2))

            act.wait_ge(s_rows, 1)
            for e in range(1, E, 2):
                c = act.value_load(counts_i[0:1, e:e + 1], min_val=0, max_val=TOKENS)
                act.dma_start(lists[bass.ds(c + e * REGION, P), :], cs[:, C_PAD:C_PAD + ROW]).then_inc(s_pad[1], 16)

            def tile_high(j, u):
                act.wait_ge(s_tx, j + 1)
                wait(act, s_gu, j - 1)
                nc.scalar.activation(xTh[:, u % 2].rearrange("p k t -> p (k t)"), p_xT[u % 2][:, 0:D],
                                     ACT.Copy).then_inc(s_xh, 1)

            def hidden_high(j, u):
                act.wait_ge(s_th, j + 1)
                wait(act, s_dn, j - 1)
                nc.scalar.activation(hTh[:, u % 2].rearrange("p k t -> p (k t)"), p_hT[u % 2][:, 0:FF],
                                     ACT.Copy).then_inc(s_hh, 1)

            def silu(j, u):
                act.wait_ge(s_gu, j + 1)
                wait(act, s_hid, j - 1)
                nc.scalar.activation(gate[:, u % 2], p_gu[u % 2][:, 0:FF], ACT.Silu).then_inc(s_sg, 1)

            def result(j, u, r):
                act.wait_ge(s_dn, j + 1)
                wait(act, s_ys[u], 16 * r)
                act.wait_ge(s_dest, j + 1)
                nc.scalar.activation(ysb[u][:], p_y[u % 2][:, 0:D], ACT.Copy, scale=gate_j[u][:, 0:1]).then_inc(s_y, 1)

            def norm_shared(j, u):
                t = j - SLOTS
                wait(act, s_tx, j - 3)
                if isinstance(j, int) and j < SLOTS + 4:
                    act.wait_ge(s_dest, j - 3)
                nc.scalar.activation(xs[u][:, 0:D], X1[:, bass.ds(t, 1)].squeeze(1), ACT.Identity,
                                     bias=ln2[:, bass.ds(t, 1), 1], scale=ln2[:, bass.ds(t, 1), 0]).then_inc(s_xsh, 1)

            tile_high(0, 0)
            tile_high(1, 1)

            def step_b(j, u, r, in_b):
                if kind(j, in_b, -1):
                    hidden_high(j - 1, (u - 1) % 4)
                if kind(j, in_b, 3) == "shared":
                    norm_shared(j + 3, (u + 3) % 4)
                if kind(j, in_b, 0):
                    silu(j, u)
                if kind(j, in_b, 2):
                    tile_high(j + 2, (u + 2) % 4)
                if kind(j, in_b, -1) == "list":
                    result(j - 1, (u - 1) % 4, r + (u - 1) // 4)

            each_tile(act, step_b)

        @block.vector
        def _(dve):
            dve.wait_ge(s_const, 16 * CONSTS)
            nc.vector.tensor_copy(low_ones[:, 0:P], cs[:, C_LOW:C_LOW + P])
            nc.vector.memset(low_ones[:, P:2 * P], 1.0)
            nc.vector.memset(before[:, 0], 0.0)
            nc.vector.tensor_copy(tagbase[:], cs[:, C_TAG:C_TAG + GS])
            nc.vector.tensor_scalar(mask[:], adj_i[:], -1.0, 1.0, ALU.mult, ALU.add).then_inc(s_prep, 1)
            dve.wait_ge(s_prep, 1)
            nc.vector.tensor_scalar(mask[:], mask[:], NEG, None, ALU.mult).then_inc(s_prep, 1)
            dve.wait_ge(s_wa, 1)
            nc.vector.tensor_copy(wext[:, :, O:O + 2],
                                  p_h[0][:, 0:2 * KD].rearrange("p (k c) -> p k c", k=KD)).then_inc(s_prep, 1)

            def split_low(m, p):
                dve.wait_ge(s_whi, m + 1)
                first = isinstance(m, int) and m == 0
                dst = shared if first else ring[:, p]
                nc.vector.tensor_tensor(dst[:, 1], wst[:], dst[:, 0].bitcast(F32), ALU.subtract).then_inc(s_wlo, 1)

            def attention(b, p, r):
                dve.wait_ge(s_nb, b + 1)
                wait(dve, s_exp, b)
                at0 = ATT_STEPS * b
                pn = p_n[:].rearrange("p (j n) -> p j n", j=GS)
                nc.vector.tensor_scalar(att[:], pn, SLOPE, None, ALU.mult).then_inc(s_att, 1)
                dve.wait_ge(s_att, at0 + 1)
                nc.vector.tensor_tensor(att[:], att[:], pn, ALU.max).then_inc(s_att, 1)
                dve.wait_ge(s_att, at0 + 2)
                nc.vector.tensor_tensor(att[:], att[:], mask[:].unsqueeze(1).to_broadcast([P, GS, P]),
                                        ALU.add).then_inc(s_att, 1)
                dve.wait_ge(s_att, at0 + 3)
                nc.vector.tensor_reduce(nmax[:], att[:], AX_X, ALU.max, negate=True).then_inc(s_att, 1)

            def stats1(c, p, r):
                wait_alone(dve, s_x[p], 16 * r + 16)
                at0 = LN1_STEPS * c
                for j in range(GS):
                    last = nc.vector.bn_stats(st[:, j], X1[:, bass.ds(4 * c + j, 1)].squeeze(1))
                last.then_inc(s_ln1, 1)
                wait_alone(dve, s_ln1, at0 + 1)
                for j in range(GS):
                    last = nc.vector.bn_aggr(mv[:, j], st[:, j])
                last.then_inc(s_ln1, 1)
                dve.wait_ge(s_ln1, at0 + 2)
                nc.vector.tensor_scalar(nw1[:, 0], mv[:, :, 1], EPS, None, ALU.add).then_inc(s_ln1, 1)

            def newton(steps, at0, nw, mean, scale, shift):
                nc.vector.scalar_tensor_tensor(nw[:, 3], nw[:, 0], -0.5, nw[:, 2], ALU.mult, ALU.mult).then_inc(steps, 1)
                dve.wait_ge(steps, at0 + 1)
                nc.vector.tensor_tensor(nw[:, 4], nw[:, 3], nw[:, 2], ALU.mult).then_inc(steps, 1)
                dve.wait_ge(steps, at0 + 2)
                nc.vector.scalar_tensor_tensor(scale, nw[:, 4], 1.5, nw[:, 2], ALU.add, ALU.mult).then_inc(steps, 1)
                dve.wait_ge(steps, at0 + 3)
                nc.vector.scalar_tensor_tensor(shift, mean, -1.0, scale, ALU.mult, ALU.mult).then_inc(steps, 1)

            def newton1(c, p, r):
                dve.wait_ge(s_ex1, 2 * c + 2)
                wait(dve, s_xn1, c - 1)
                newton(s_ln1, LN1_STEPS * c + 3, nw1, mv[:, :, 0], ln1[:, p, :, 0], ln1[:, p, :, 1])

            def add_graph(b, p, r):
                dve.wait_ge(s_out, b + 1)
                at0 = X1_STEPS * b
                nc.vector.reciprocal(rsum[:], psums[:]).then_inc(s_x1, 1)
                dve.wait_ge(s_x1, at0 + 1)
                for j in range(GS):
                    xt = X1[:, bass.ds(4 * b + j, 1), 0:O].squeeze(1)
                    nc.vector.scalar_tensor_tensor(xt, p_o[:, j * O:(j + 1) * O], rsum[:, j:j + 1], xt,
                                                   ALU.mult, ALU.add)
                xh = X1[:, bass.ds(4 * b, GS), O:D]
                nc.vector.tensor_tensor(xh, xh, hsb[:, p, :, 0:O], ALU.add).then_inc(s_x1, 1)
                wait_alone(dve, s_x1, at0 + 2)
                for j in range(GS):
                    last = nc.vector.bn_stats(st2[:, j], X1[:, bass.ds(4 * b + j, 1)].squeeze(1))
                last.then_inc(s_x1, 1)
                wait_alone(dve, s_x1, at0 + 3)
                for j in range(GS):
                    last = nc.vector.bn_aggr(mv2[:, j], st2[:, j])
                last.then_inc(s_x1, 1)
                dve.wait_ge(s_x1, at0 + 4)
                nc.vector.tensor_scalar(nw2[:, 0], mv2[:, :, 1], EPS, None, ALU.add).then_inc(s_x1, 1)

            def norm2(b, p, r):
                dve.wait_ge(s_ex2, 2 * b + 2)
                at0 = X1_STEPS * b + 5
                newton(s_x1, at0, nw2, mv2[:, :, 0], ln2[:, bass.ds(4 * b, GS), 0], ln2[:, bass.ds(4 * b, GS), 1])
                dve.wait_ge(s_x1, at0 + 4)
                wait(dve, s_scat[p], 16 * GROUP_SCATTERS * r)
                for j in range(GS):
                    t = 4 * b + j
                    last = nc.vector.tensor_scalar(x2[p][:, j, 0:D], X1[:, bass.ds(t, 1)].squeeze(1),
                                                   ln2[:, bass.ds(t, 1), 0], ln2[:, bass.ds(t, 1), 1],
                                                   ALU.mult, ALU.add)
                last.then_inc(s_x1, 1)

            def route(a, p, r):
                at0 = ROUTE_STEPS * a
                dve.wait_ge(s_ez, a + 1)
                nc.vector.tensor_scalar(aff1[:], ez[:], 1.0, None, ALU.add).then_inc(s_rt, 1)
                dve.wait_ge(s_rt, at0 + 1)
                nc.vector.reciprocal(aff[:], aff1[:]).then_inc(s_rt, 1)
                dve.wait_ge(s_rt, at0 + 2)
                nc.vector.tensor_tensor(score[:], aff[:], bias_s[:].unsqueeze(1).to_broadcast([P, GS, E]),
                                        ALU.add).then_inc(s_rt, 1)
                wait_alone(dve, s_rt, at0 + 3)
                for j in range(GS):
                    last = nc.vector.max(top8[:, j], score[:, j])
                last.then_inc(s_rt, 1)
                wait_alone(dve, s_rt, at0 + 4)
                for j in range(GS):
                    last = nc.vector.max_index(topi[:, j], top8[:, j], score[:, j])
                last.then_inc(s_rt, 1)
                dve.wait_ge(s_rt, at0 + 5)
                nc.vector.tensor_copy(topf[:], topi[:, :, 0:TOP]).then_inc(s_rt, 1)
                dve.wait_ge(s_rt, at0 + 6)
                iota = cs[:, C_IOTA:C_IOTA + E].unsqueeze(1).to_broadcast([P, TOP, E])
                for j in range(GS):
                    last = nc.vector.tensor_tensor(onehot[:, j], topf[:, j].unsqueeze(2).to_broadcast([P, TOP, E]),
                                                   iota, ALU.is_equal)
                last.then_inc(s_rt, 1)
                dve.wait_ge(s_rt, at0 + 7)
                with nc.allow_low_precision("zeros and ones"):
                    nc.vector.tensor_reduce(taken[:], onehot[:].rearrange("p j k e -> p j e k"), AX_X,
                                            ALU.add).then_inc(s_rt, 1)
                dve.wait_ge(s_rt, at0 + 8)
                nc.vector.tensor_tensor(sel[:], taken[:], aff[:], ALU.mult)
                nc.vector.scalar_tensor_tensor(tag1[:], onehot[:, :, 2], 2.0, taken[:], ALU.mult,
                                               ALU.add).then_inc(s_rt, 1)
                dve.wait_ge(s_rt, at0 + 9)
                nc.vector.tensor_tensor(tag2[:], tag1[:], onehot[:, :, 1], ALU.add)
                nc.vector.tensor_reduce(den[:, 0], sel[:], AX_X, ALU.add).then_inc(s_rt, 1)
                dve.wait_ge(s_rt, at0 + 10)
                nc.vector.tensor_tensor(x2[p][:, :, TAG:GATE], tag2[:],
                                        tagbase[:].unsqueeze(2).to_broadcast([P, GS, E]), ALU.add)
                nc.vector.tensor_scalar(den[:, 1], den[:, 0], 1e-9, None, ALU.add).then_inc(s_rt, 1)
                dve.wait_ge(s_rt, at0 + 11)
                nc.vector.tensor_scalar(tagbase[:], tagbase[:], float(TOP * GS * P), None, ALU.add)
                nc.vector.tensor_reduce(newly[:], taken[:].rearrange("p j e -> p e j"), AX_X, ALU.add)
                nc.vector.reciprocal(den[:, 2], den[:, 1]).then_inc(s_rt, 1)
                dve.wait_ge(s_rt, at0 + 12)
                with nc.allow_low_precision("whole numbers up to 64"):
                    nc.vector.tensor_tensor(before[:, 1 - p], before[:, p], newly[:], ALU.add)
                nc.vector.tensor_tensor(x2[p][:, :, GATE:ROW], aff[:], den[:, 2].unsqueeze(2).to_broadcast([P, GS, E]),
                                        ALU.mult).then_inc(s_rt, 1)

            def positions(a, p, r):
                at0 = POS_STEPS * a
                dve.wait_ge(s_rk, a + 1)
                nc.vector.tensor_tensor(rankb[:], p_rk.rearrange("p (j e) -> p j e", j=GS),
                                        cs[:, C_BASE:C_BASE + E].unsqueeze(1).to_broadcast([P, GS, E]),
                                        ALU.add).then_inc(s_pos, 1)
                dve.wait_ge(s_pos, at0 + 1)
                for j in range(GS):
                    last = nc.vector.tensor_tensor(selpos[:, j], onehot[:, j],
                                                   rankb[:, j].unsqueeze(1).to_broadcast([P, TOP, E]), ALU.mult)
                last.then_inc(s_pos, 1)
                dve.wait_ge(s_pos, at0 + 2)
                nc.vector.tensor_reduce(posf[:], selpos[:], AX_X, ALU.add).then_inc(s_pos, 1)
                dve.wait_ge(s_pos, at0 + 3)
                nc.vector.tensor_copy(pos[p][:], posf[:].rearrange("p j k -> p (j k)")).then_inc(s_pos, 1)

            def split_next(n, p, r):
                split_low(n + 1, p)

            split_low(0, 0)
            stages(dve, (1, attention), (3, stats1), (0, route), (3, newton1), (1, add_graph), (0, positions),
                   (0, split_next), (1, norm2))

            dve.wait_ge(s_cnt, 1)
            nc.vector.tensor_copy(cnt[:], bank[7][:, 0:E]).then_inc(s_tb, 1)
            dve.wait_ge(s_tb, 1)
            nc.vector.tensor_scalar(ntf[:], cnt[:], 1.0 / P, (P - 1) / 2 / P, ALU.mult, ALU.add).then_inc(s_tb, 1)
            nc.vector.tensor_copy(counts_i[:], cnt[0:1, :])
            dve.wait_ge(s_tb, 2)
            nc.vector.tensor_copy(nti[:], ntf[:]).then_inc(s_tb, 1)
            dve.wait_ge(s_tb, 3)
            nc.vector.tensor_scalar(ntf[:], nti[:], 1.0, None, ALU.max).then_inc(s_tb, 1)
            dve.wait_ge(s_tb, 4)
            nc.vector.tensor_tensor_scan(cum[:], cs[:, C_ONE:C_ONE + E], ntf[:], 0.0, ALU.mult, ALU.add)\
                .then_inc(s_tb, 1)
            dve.wait_ge(s_tb, 5)
            jt = cs[:, C_TILE:C_TILE + 2]
            nc.vector.tensor_tensor(ended[:], cum[:].unsqueeze(1).to_broadcast([P, 2, E]),
                                    jt.unsqueeze(2).to_broadcast([P, 2, E]), ALU.is_le).then_inc(s_tb, 1)
            dve.wait_ge(s_tb, 6)
            nc.vector.tensor_reduce(ej[:, 0], ended[:], AX_X, ALU.add)
            nc.vector.tensor_tensor(tmp2[:], ended[:], ntf[:].unsqueeze(1).to_broadcast([P, 2, E]),
                                    ALU.mult).then_inc(s_tb, 1)
            dve.wait_ge(s_tb, 7)
            nc.vector.tensor_reduce(ej[:, 1], tmp2[:], AX_X, ALU.add).then_inc(s_tb, 1)
            dve.wait_ge(s_tb, 8)
            nc.vector.tensor_tensor(ej[:, 2], jt, ej[:, 1], ALU.subtract)
            nc.vector.tensor_tensor(ej[:, 3], jt, ej[:, 1], ALU.is_equal)
            nc.vector.tensor_scalar(ej[:, 4], ej[:, 0], float(REGION), None, ALU.mult)
            nc.vector.tensor_scalar(ej[:, 6], ej[:, 0], float(E - RING), None, ALU.is_le)
            nc.vector.tensor_scalar(tv[:, 0], ej[:, 0], float(E - 1), None, ALU.min).then_inc(s_tb, 1)
            dve.wait_ge(s_tb, 9)
            nc.vector.scalar_tensor_tensor(ej[:, 5], ej[:, 2], float(P), ej[:, 4], ALU.mult, ALU.add)
            nc.vector.tensor_tensor(tv[:, 2], ej[:, 3], ej[:, 6], ALU.mult).then_inc(s_tb, 1)
            dve.wait_ge(s_tb, 10)
            nc.vector.tensor_scalar(tv[:, 1], ej[:, 5], float(E * REGION), None, ALU.min).then_inc(s_tb, 1)
            dve.wait_ge(s_tb, 12)
            nc.vector.tensor_copy(table[:, 0:2].rearrange("p v j -> p (v j)"), bank[6][0:1, :])
            nc.vector.tensor_copy(table[:, 2], bank[5][0:1, 0:2 * P]).then_inc(s_rows, 1)

            def tile_low(j, u):
                dve.wait_ge(s_xh, j + 1)
                nc.vector.tensor_tensor(xTl[:, u % 2].rearrange("p k t -> p (k t)"), p_xT[u % 2][:, 0:D],
                                        xTh[:, u % 2].rearrange("p k t -> p (k t)").bitcast(F32),
                                        ALU.subtract).then_inc(s_xlo, 1)

            def hidden_low(j, u):
                dve.wait_ge(s_hh, j + 1)
                nc.vector.tensor_tensor(hTl[:, u % 2].rearrange("p k t -> p (k t)"), p_hT[u % 2][:, 0:FF],
                                        hTh[:, u % 2].rearrange("p k t -> p (k t)").bitcast(F32),
                                        ALU.subtract).then_inc(s_hl, 1)

            def multiply(j, u):
                dve.wait_ge(s_sg, j + 1)
                wait(dve, s_th, j - 1)
                nc.vector.tensor_tensor(hid[:, u % 2], p_gu[u % 2][:, FF:WIDE], gate[:, u % 2],
                                        ALU.mult).then_inc(s_hid, 1)

            def finish(j, u):
                t = j - SLOTS
                xt = X1[:, bass.ds(t, 1)].squeeze(1)
                dve.wait_ge(s_acc, (TOP - 1) * (t + 1))
                dve.wait_ge(s_xsh, t + 1)
                nc.vector.tensor_tensor(xt, yr[:, u, 0:D], xt, ALU.add).then_inc(s_fin, 1)
                dve.wait_ge(s_fin, 2 * t + 1)
                dve.wait_ge(s_dn, j + 1)
                nc.vector.tensor_tensor(xt, p_y[u % 2][:, 0:D], xt, ALU.add).then_inc(s_fin, 1)

            tile_low(0, 0)
            tile_low(1, 1)

            def step_b(j, u, r, in_b):
                if kind(j, in_b, -1):
                    hidden_low(j - 1, (u - 1) % 4)
                if kind(j, in_b, 0):
                    multiply(j, u)
                if kind(j, in_b, 2):
                    tile_low(j + 2, (u + 2) % 4)
                if kind(j, in_b, -1) == "shared":
                    finish(j - 1, (u - 1) % 4)

            each_tile(dve, step_b)

        @block.tensor
        def _(pe):
            pe.wait_ge(s_const, 16 * CONSTS)
            for k in range(KD):
                last = nc.tensor.matmul(p_h[0][:, 2 * k:2 * k + 2], wts[:, k * P:(k + 1) * P], ats[:],
                                        start=True, stop=True)
            last.then_inc(s_wa, 1)
            pe.wait_ge(s_prep, 3)

            def score_sums(b, p, r):
                pe.wait_ge(s_hsb, b + 1)
                wait(pe, s_att, ATT_STEPS * (b - 1) + 2)
                for j in range(GS):
                    dst = p_n[:, j * P:(j + 1) * P]
                    nc.tensor.matmul(dst, hsb[:, p, j, O + 1:O + 2].to_broadcast([P, P]), ident, start=True, stop=False)
                    last = nc.tensor.matmul(dst, ident, hsb[:, p, j, O:O + 1].to_broadcast([P, P]),
                                            start=False, stop=True)
                last.then_inc(s_nb, 1)

            def transpose_prob(b, p, r):
                pe.wait_ge(s_exp, b + 1)
                wait(pe, s_pT, b)
                for j in range(GS):
                    last = nc.tensor.transpose(p_pt[:, j * P:(j + 1) * P], prob[:, j], ident)
                last.then_inc(s_tp, 1)

            def transpose_xn1(c, p, r):
                pe.wait_ge(s_xn1, c + 1)
                wait(pe, s_x2T, c - 1)
                wait(pe, s_xnT, c)
                for k in range(KD):
                    for j in range(GS):
                        last = nc.tensor.transpose(p_t[k][:, j * P:(j + 1) * P], xn1[:, p, j, k * P:(k + 1) * P], ident)
                last.then_inc(s_t1, 1)

            def attend(b, p, r):
                pe.wait_ge(s_pT, b + 1)
                wait(pe, s_x1, X1_STEPS * (b - 1) + 2)
                for j in range(GS):
                    last = nc.tensor.matmul(p_o[:, j * O:(j + 1) * O], probT[:, j], hsb[:, p, j, 0:O],
                                            start=True, stop=True)
                last.then_inc(s_out, 1)

            def ranks(a, p, r):
                pe.wait_ge(s_rt, ROUTE_STEPS * a + 8)
                nc.tensor.matmul(p_rk, lower, taken[:].rearrange("p j e -> p (j e)"), start=True, stop=False)
                for j in range(GS - 1):
                    n = GS - 1 - j
                    nc.tensor.matmul(p_rk[:, (j + 1) * E:].rearrange("p (j e) -> p j e", j=n), ones,
                                     taken[:, j:j + 1].to_broadcast([P, n, E]), start=False, stop=False)
                nc.tensor.matmul(p_rk.rearrange("p (j e) -> p j e", j=GS), ones,
                                 before[:, p:p + 1].to_broadcast([P, GS, E]), start=False, stop=True).then_inc(s_rk, 1)

            def project(c, p, r):
                pe.wait_ge(s_xnT, c + 1)
                wait(pe, s_hsb, c)
                for j in range(GS):
                    for k in range(KD):
                        last = nc.tensor.matmul(p_h[j // 2][:, (j % 2) * (O + 2):(j % 2 + 1) * (O + 2)],
                                                xnT[:, k, j * P:(j + 1) * P], wext[:, k],
                                                start=(k == 0), stop=(k == KD - 1))
                last.then_inc(s_h, 1)

            def transpose_x2(b, p, r):
                pe.wait_ge(s_x1, X1_STEPS * b + X1_STEPS)
                pe.wait_ge(s_xnT, b + 2) if not isinstance(b, int) or b < GROUPS - 1 else None
                for k in range(KD):
                    for j in range(GS):
                        last = nc.tensor.transpose(p_t[k][:, j * P:(j + 1) * P], x2[p][:, j, k * P:(k + 1) * P], ident)
                last.then_inc(s_t2, 1)

            def logits(b, p, r):
                pe.wait_ge(s_x2T, b + 1)
                wait(pe, s_ez, b)
                for j in range(GS):
                    for k in range(KD):
                        last = nc.tensor.matmul(p_lg[:, j * E:(j + 1) * E], x2T[:, k, j * P:(j + 1) * P], gws[:, k],
                                                start=(k == 0), stop=(k == KD - 1))
                last.then_inc(s_lg, 1)

            stages(pe, (1, score_sums), (0, transpose_x2), (0, logits), (2, transpose_xn1), (1, transpose_prob),
                   (2, project), (1, attend), (0, ranks))

            pe.wait_ge(s_rt, ROUTE_STEPS * GROUPS)
            pe.wait_ge(s_pos, POS_STEPS * GROUPS)
            nc.tensor.matmul(bank[7][:, 0:E], ones, before[:, GROUPS % 2], start=True, stop=True).then_inc(s_cnt, 1)
            pe.wait_ge(s_tb, 11)
            for v in range(3):
                for h in range(2):
                    dst = bank[6][0:1, v * 2 * P + h * P:v * 2 * P + h * P + P] if v < 2 else bank[5][0:1, h * P:h * P + P]
                    last = nc.tensor.matmul(dst, tv[:, v, h:h + 1], ident, start=True, stop=True)
            last.then_inc(s_tb, 1)
            pe.wait_ge(s_rows, 1)

            def transpose_tile(j, u, r, what):
                if what == "list":
                    pe.wait_ge(s_xl[u], 16 * r + 16)
                else:
                    pe.wait_ge(s_xsh, j - SLOTS + 1)
                wait(pe, s_xlo, j - 1)
                for k in range(KD):
                    last = nc.tensor.transpose(p_xT[u % 2][:, k * P:(k + 1) * P], xs[u][:, k * P:(k + 1) * P], ident)
                last.then_inc(s_tx, 1)

            def expert(j, what):
                if what == "shared":
                    return shared[:, 0], shared[:, 1]
                e = pe.value_load(table[0:1, 0, bass.ds(j, 1)], min_val=0, max_val=E - 1)
                pe.wait_ge(s_w, 16 * (e + 1))
                slot = bass.ds(e % RING, 1)
                return ring[:, slot, 0].squeeze(1), ring[:, slot, 1].squeeze(1)

            def products(dst, xh, xl, wh, wl, width, at0, n):
                for k in range(n):
                    cols = slice(at0 + k * width, at0 + (k + 1) * width)
                    nc.tensor.matmul(dst, xh[:, k], wh[:, cols], start=(k == 0), stop=False)
                    nc.tensor.matmul(dst, xh[:, k], wl[:, cols], start=False, stop=False)
                    last = nc.tensor.matmul(dst, xl[:, k], wh[:, cols], start=False, stop=(k == n - 1))
                return last

            def gate_up(j, u, what):
                wh, wl = expert(j, what)
                pe.wait_ge(s_xlo, j + 1)
                wait(pe, s_hid, j - 1)
                products(p_gu[u % 2][:, 0:WIDE], xTh[:, u % 2], xTl[:, u % 2], wh, wl, WIDE, 0, KD).then_inc(s_gu, 1)

            def transpose_hidden(j, u):
                pe.wait_ge(s_hid, j + 1)
                wait(pe, s_hl, j - 1)
                for k in range(KF):
                    last = nc.tensor.transpose(p_hT[u % 2][:, k * P:(k + 1) * P], hid[:, u % 2, k * P:(k + 1) * P], ident)
                last.then_inc(s_th, 1)

            def down(j, u, what, before_that):
                wh, wl = expert(j, what)
                pe.wait_ge(s_hl, j + 1)
                if before_that == "list":
                    wait(pe, s_y, j - 1)
                elif before_that == "shared":
                    wait(pe, s_fin, 2 * (j - 1 - SLOTS))
                products(p_y[u % 2][:, 0:D], hTh[:, u % 2], hTl[:, u % 2], wh, wl, D, KD * WIDE, KF).then_inc(s_dn, 1)

            transpose_tile(0, 0, 0, "list")
            transpose_tile(1, 1, 0, "list")

            def step_b(j, u, r, in_b):
                if kind(j, in_b, -1):
                    transpose_hidden(j - 1, (u - 1) % 4)
                if kind(j, in_b, 0):
                    gate_up(j, u, kind(j, in_b, 0))
                if kind(j, in_b, 2):
                    transpose_tile(j + 2, (u + 2) % 4, r + (u + 2) // 4, kind(j, in_b, 2))
                if kind(j, in_b, -1):
                    down(j - 1, (u - 1) % 4, kind(j, in_b, -1), kind(j, in_b, -3))

            each_tile(pe, step_b)


def kernel(x, adj, L0_gnn_W, L0_gnn_a, L0_ffn_gate_w, L0_ffn_expert_bias, L0_ffn_shared_gate_up,
           L0_ffn_shared_down, L0_ffn_expert_gate_up, L0_ffn_expert_down):
    import numpy as np
    import concourse.bacc as bacc
    from concourse.bass_utils import run_bass_kernel_spmd

    def chunks(a):
        n, kp, m = a.shape
        return a.reshape(n, kp // P, P, m).transpose(0, 2, 1, 3).reshape(n, P, -1)

    gate_up = np.concatenate([np.asarray(L0_ffn_shared_gate_up)[None], np.asarray(L0_ffn_expert_gate_up)])
    down = np.concatenate([np.asarray(L0_ffn_shared_down)[None], np.asarray(L0_ffn_expert_down)])
    weights = np.concatenate([chunks(gate_up.transpose(0, 2, 1)), chunks(down.transpose(0, 2, 1))], axis=2)
    w = np.asarray(L0_gnn_W)
    arrays = {
        "x": np.asarray(x),
        "adj": np.asarray(adj),
        "w": chunks(w[None])[0].reshape(P, KD, O),
        "wt": w.T,
        "at": np.asarray(L0_gnn_a)[:, :, 0].T,
        "gate_wt": chunks(np.asarray(L0_ffn_gate_w).T[None])[0].reshape(P, KD, E),
        "bias": np.broadcast_to(np.asarray(L0_ffn_expert_bias), (P, E)),
        "weights": weights,
        "consts": constants(),
    }
    arrays = {f"in_{k}": np.ascontiguousarray(v) for k, v in arrays.items()}
    nc = bacc.Bacc("TRN2", target_bir_lowering=False, num_devices=1)
    aps = [nc.dram_tensor(k, v.shape, mybir.dt.from_np(v.dtype), kind="ExternalInput").ap() for k, v in arrays.items()]
    out = nc.dram_tensor("out_0", (TILES, P, D), F32, kind="ExternalOutput").ap()
    build(nc, *aps, out)
    r = run_bass_kernel_spmd(nc, [arrays], core_ids=[0])
    return r.results[0]["out_0"]
```

```python
from contextlib import ExitStack

import concourse.bass as bass
from concourse import mybir

ALU = mybir.AluOpType
ACT = mybir.ActivationFunctionType
AX_X = mybir.AxisListType.X
F32 = mybir.dt.float32
F32R = mybir.dt.float32r
BF16 = mybir.dt.bfloat16
I32 = mybir.dt.int32
U32 = mybir.dt.uint32

P = 128
TILES = 64
TOKENS = TILES * P
D = 256
KD = D // P
O = 128
FF = 256
KF = FF // P
E = 16
TOP = 3
EPS = 1e-5
SLOPE = 0.2
NEG = -1e9

GS = 4
GROUPS = TILES // GS

REGION = TOKENS + P
TAG, GATE = D, D + E
ROW = D + 2 * E
LIST_ROWS = E * REGION + P
NO_ROW = 4 * TOKENS * TOP

SLOTS = (TOKENS * TOP + E * (P - 1)) // P
SLOTS += -SLOTS % 4
WIDE = 2 * FF
WX = KD * WIDE + KF * D
RING = 4

C_ID, C_LOW = 0, P
C_IOTA = 2 * P
C_BASE = C_IOTA + E
C_TAG = C_BASE + E
C_TILE = C_TAG + GS
C_PAD = C_TILE + 2
C_ONE = C_PAD + ROW
C_MOVE = C_ONE + E
C_ALL = C_MOVE + E

LN1_STEPS, ATT_STEPS, X1_STEPS, ROUTE_STEPS, POS_STEPS = 7, 3, 9, 13, 4
GROUP_SCATTERS = GS * TOP


def constants():
    import numpy as np

    c = np.zeros((P, C_ALL), np.float32)
    p = np.arange(P)
    c[:, C_ID:C_ID + P] = np.eye(P)
    c[:, C_LOW:C_LOW + P] = p[:, None] < p[None, :]
    c[:, C_IOTA:C_IOTA + E] = np.arange(E)
    c[:, C_BASE:C_BASE + E] = np.arange(E) * REGION
    c[:, C_TAG:C_TAG + GS] = TOP * (P * np.arange(GS)[None, :] + p[:, None]) - 1
    c[:, C_TILE:C_TILE + 2] = P * np.arange(2)[None, :] + p[:, None]
    c[:, C_PAD + TAG:C_PAD + GATE] = NO_ROW
    c[:, C_ONE:C_ONE + E] = 1.0
    place = 2 * WX * (np.arange(E + 1) % RING)
    c[:, C_MOVE:C_MOVE + E] = place[1:] - place[:-1]
    return c


def build(nc, x, adj, w, wt, at, gate_wt, bias, weights, consts, out):
    with ExitStack() as ctx:
        def sb(name, shape, dt):
            return ctx.enter_context(nc.sbuf_tensor(name, shape, dt))

        def sem(name):
            return ctx.enter_context(nc.semaphore(name))

        def wait(eng, s, value):
            if not (isinstance(value, int) and value <= 0):
                eng.wait_ge(s, value)

        def wait_alone(eng, s, value):
            value = value if isinstance(value, int) else eng.to_reg(value)
            eng.wait_ge(s_const, 16 * CONSTS)
            eng.wait_ge(s, value)

        lists = nc.dram_tensor("lists", [LIST_ROWS, ROW], F32).ap()
        split_w = nc.dram_tensor("split_w", [E, P, 2, WX], F32).ap()
        routed = nc.dram_tensor("routed", [TOKENS * TOP, D], F32).ap()
        routed_t = routed.rearrange("(t p k) d -> t p (k d)", p=P, k=TOP)

        X1 = sb("X1", [P, TILES, D], F32)
        ln2 = sb("ln2", [P, TILES, 2], F32)
        cs = sb("cs", [P, C_ALL], F32)
        ident = cs[:, C_ID:C_ID + P]
        ring = sb("ring", [P, RING, 2, WX], F32R)
        shared = sb("shared", [P, 2, WX], F32R)
        table = sb("table", [1, 4, 2 * P], I32)
        counts_i = sb("counts_i", [1, E], I32)

        wext = sb("wext", [P, KD, O + 2], F32)
        wts = sb("wts", [P, D], F32)
        ats = sb("ats", [P, 2], F32)
        gws = sb("gws", [P, KD, E], F32)
        bias_s = sb("bias_s", [P, E], F32)
        adj_i = sb("adj_i", [P, P], I32)
        mask = sb("mask", [P, P], F32)
        low_ones = sb("low_ones", [P, 2 * P], BF16)
        lower, ones = low_ones[:, 0:P], low_ones[:, P:2 * P]
        wst = sb("wst", [P, WX], F32)
        st = sb("st", [P, GS, 6], F32)
        mv = sb("mv", [P, GS, 2], F32)
        nw1 = sb("nw1", [P, 5, GS], F32)
        ln1 = sb("ln1", [P, 2, GS, 2], F32)
        st2 = sb("st2", [P, GS, 6], F32)
        mv2 = sb("mv2", [P, GS, 2], F32)
        nw2 = sb("nw2", [P, 5, GS], F32)
        xn1 = sb("xn1", [P, 2, GS, D], F32)
        xnT = sb("xnT", [P, KD, GS * P], F32)
        hsb = sb("hsb", [P, 2, GS, O + 2], F32)
        att = sb("att", [P, GS, P], F32)
        nmax = sb("nmax", [P, GS], F32)
        prob = sb("prob", [P, GS, P], F32)
        psums = sb("psums", [P, GS], F32)
        rsum = sb("rsum", [P, GS], F32)
        probT = sb("probT", [P, GS, P], F32)
        x2 = [sb(f"x2_{i}", [P, GS, ROW], F32) for i in range(2)]
        x2T = sb("x2T", [P, KD, GS * P], F32)
        tagbase = sb("tagbase", [P, GS], F32)
        ez = sb("ez", [P, GS, E], F32)
        aff1 = sb("aff1", [P, GS, E], F32)
        aff = sb("aff", [P, GS, E], F32)
        score = sb("score", [P, GS, E], F32)
        top8 = sb("top8", [P, GS, 8], F32)
        topi = sb("topi", [P, GS, 8], U32)
        topf = sb("topf", [P, GS, TOP], F32)
        onehot = sb("onehot", [P, GS, TOP, E], F32)
        taken = sb("taken", [P, GS, E], BF16)
        tag1 = sb("tag1", [P, GS, E], F32)
        tag2 = sb("tag2", [P, GS, E], F32)
        sel = sb("sel", [P, GS, E], F32)
        den = sb("den", [P, 3, GS], F32)
        before = sb("before", [P, 2, E], BF16)
        newly = sb("newly", [P, E], F32)
        rankb = sb("rankb", [P, GS, E], F32)
        selpos = sb("selpos", [P, GS, TOP, E], F32)
        posf = sb("posf", [P, GS, TOP], F32)
        pos = [sb(f"pos_{i}", [P, GS * TOP], I32) for i in range(2)]

        cnt = sb("cnt", [P, E], F32)
        nti = sb("nti", [P, E], I32)
        ntf = sb("ntf", [P, E], F32)
        cum = sb("cum", [P, E], F32)
        ended = sb("ended", [P, 2, E], F32)
        tmp2 = sb("tmp2", [P, 2, E], F32)
        ej = sb("ej", [P, 8, 2], F32)
        tv = sb("tv", [P, 4, 2], F32)
        tmp3 = sb("tmp3", [P, 2, E], F32)

        xs = [sb(f"xs_{i}", [P, ROW], F32) for i in range(4)]
        gate_j = [sb(f"gate_j_{i}", [P, 1], F32) for i in range(4)]
        dest = [sb(f"dest_{i}", [P, 1], I32) for i in range(4)]
        xTh = sb("xTh", [P, 2, KD, P], F32R)
        xTl = sb("xTl", [P, 2, KD, P], F32R)
        gate = sb("gate", [P, 2, FF], F32)
        hid = sb("hid", [P, 2, FF], F32)
        hTh = sb("hTh", [P, 2, KF, P], F32R)
        hTl = sb("hTl", [P, 2, KF, P], F32R)
        ysb = [sb(f"ysb_{i}", [P, D], F32) for i in range(4)]
        yr = ring[:, 0].rearrange("p h c -> p (h c)").bitcast(F32).rearrange("p (u c) -> p u c", u=4)

        bank = [ctx.enter_context(nc.psum_tensor(f"bank{i}", [P, 512], F32)) for i in range(8)]
        p_t = bank[0:2]
        p_h = bank[2:4]
        p_n, p_pt, p_o = bank[4], bank[4], bank[6]
        p_lg = bank[7][:, 0:GS * E]
        p_rk = bank[5][:, 0:GS * E]
        p_xT, p_gu, p_hT, p_y = bank[0:2], bank[2:4], bank[4:6], bank[6:8]

        s_const = sem("const_loaded")
        s_x = [sem(f"x_loaded{i}") for i in range(2)]
        s_wa = sem("wa_product")
        s_prep = sem("vector_prepared")
        s_win = sem("weights_in")
        s_whi = sem("weights_high")
        s_wlo = sem("weights_low")
        s_wout = [sem(f"weights_out{i}") for i in range(2)]
        s_ln1 = sem("ln1_steps")
        s_ex1 = sem("guess1_steps")
        s_ex2 = sem("guess2_steps")
        s_xn1 = sem("xn1_ready")
        s_t1 = sem("xn1_transposed")
        s_xnT = sem("xnT_ready")
        s_h = sem("h_product")
        s_hsb = sem("h_ready")
        s_nb = sem("neighbour_rows")
        s_slope = sem("scores_sloped")
        s_att = sem("attention_steps")
        s_exp = sem("prob_ready")
        s_tp = sem("prob_transposed")
        s_pT = sem("probT_ready")
        s_out = sem("attended")
        s_x1 = sem("x1_steps")
        s_x2 = sem("x2_ready")
        s_t2 = sem("x2_transposed")
        s_x2T = sem("x2T_ready")
        s_lg = sem("logits")
        s_ez = sem("exp_logits")
        s_rt = sem("route_steps")
        s_rk = sem("ranks")
        s_pos = sem("position_steps")
        s_scat = [sem(f"scattered{i}") for i in range(2)]
        s_cnt = sem("counts")
        s_tb = sem("table_steps")
        s_rows = sem("table_rows")
        s_pad = [sem(f"padded{i}") for i in range(2)]
        s_xl = [sem(f"list_tile_loaded{i}") for i in range(4)]
        s_w = sem("expert_weights_loaded")
        s_xsh = sem("shared_tile_ready")
        s_tx = sem("tile_transposed")
        s_xh = sem("tile_high")
        s_xlo = sem("tile_low")
        s_gu = sem("gate_up")
        s_sg = sem("gate_ready")
        s_hid = sem("hidden_ready")
        s_th = sem("hidden_transposed")
        s_hh = sem("hidden_high")
        s_hl = sem("hidden_low")
        s_dn = sem("down")
        s_y = sem("result_ready")
        s_dest = sem("dest_ready")
        s_ys = [sem(f"result_scattered{i}") for i in range(4)]
        s_yl = [sem(f"routed_loaded{i}") for i in range(4)]
        s_acc = sem("routed_added")
        s_fin = sem("tile_finished")
        s_store = sem("stored")

        CONSTS = 7
        xg = x.rearrange("(g j) p d -> g p j d", j=GS)

        def each_group(eng, body):
            for n in range(-4, 2):
                body(n, n % 2, n // 2)
            with eng.Fori(1, (GROUPS - 4) // 2) as i:
                body(2 * i, 0, i)
                body(2 * i + 1, 1, i)
            for n in range(GROUPS - 4, GROUPS):
                body(n, n % 2, n // 2)

        def ahead(n, p, r, lag):
            if isinstance(n, int) and not 0 <= n + lag < GROUPS:
                return None
            return n + lag, (p + lag) % 2, r + (p + lag) // 2

        def stages(eng, *parts):
            def step(n, p, r):
                for lag, part in parts:
                    g = ahead(n, p, r, lag)
                    if g is not None:
                        part(*g)
            each_group(eng, step)

        DRAIN = 3

        def each_tile(eng, body):
            total = SLOTS + TILES
            for j in range(0, 8):
                body(j, j % 4, j // 4, True)
            with eng.Fori(2, SLOTS // 4 - 1) as i:
                for u in range(4):
                    body(4 * i + u, u, i, True)
            for j in range(SLOTS - 4, SLOTS + 4):
                body(j, j % 4, j // 4, j < SLOTS)
            with eng.Fori(SLOTS // 4 + 1, total // 4 - 1) as i:
                for u in range(4):
                    body(4 * i + u, u, i, False)
            for j in range(total - 4, total + DRAIN):
                body(j, j % 4, j // 4, False)

        def kind(j, in_b, lag):
            if not isinstance(j, int):
                return "list" if in_b else "shared"
            return "list" if 0 <= j + lag < SLOTS else "shared" if SLOTS <= j + lag < SLOTS + TILES else None

        block = ctx.enter_context(nc.Block())

        @block.sync
        def _(sp):
            for dst, src in ((cs[:], consts), (wts[:], wt), (ats[:], at), (gws[:], gate_wt), (bias_s[:], bias),
                             (adj_i[:], adj), (wext[:, :, 0:O], w)):
                sp.dma_start(dst, src).then_inc(s_const, 16)

            def load_x(c, p, r):
                wait(sp, s_x[p], 16 * r)
                sp.dma_start(X1[:, bass.ds(4 * c, 4), :], xg[bass.ds(c, 1)].squeeze(0)).then_inc(s_x[p], 16)

            def load_weights(m):
                wait(sp, s_wlo, m)
                sp.dma_start(wst[:], weights[bass.ds(m, 1)].squeeze(0)).then_inc(s_win, 16)

            def store_weights(e, p, r):
                sp.wait_ge(s_whi, e + 2)
                sp.wait_ge(s_wlo, e + 2)
                sp.dma_start(split_w[bass.ds(e, 1)].squeeze(0), ring[:, p].bitcast(F32)).then_inc(s_wout[p], 16)

            for c in range(4):
                load_x(c, c % 2, c // 2)
            load_weights(0)
            with sp.Fori(2, GROUPS // 2) as i:
                for p in range(2):
                    load_x(2 * i + p, p, i)

            def expert_weights(n, p, r):
                load_weights(n + 1)
                store_weights(n, p, r)

            stages(sp, (0, expert_weights))

            sp.wait_ge(s_rows, 1)
            pad = cs[:, C_PAD:C_PAD + ROW]
            sp.dma_start(lists[E * REGION:E * REGION + P, :], pad).then_inc(s_pad[0], 16)
            for e in range(0, E, 2):
                c = sp.value_load(counts_i[0:1, e:e + 1], min_val=0, max_val=TOKENS)
                sp.dma_start(lists[bass.ds(c + e * REGION, P), :], pad).then_inc(s_pad[0], 16)
            sp.wait_ge(s_wout[0], 16 * (E // 2))
            sp.wait_ge(s_wout[1], 16 * (E // 2))
            for e in range(RING - 1):
                wait(sp, s_w, 16 * e)
                sp.dma_start(ring[:, e].bitcast(F32), split_w[e]).then_inc(s_w, 16)
            sp.wait_ge(s_scat[0], 16 * GROUP_SCATTERS * (GROUPS // 2))
            sp.wait_ge(s_scat[1], 16 * GROUP_SCATTERS * (GROUPS // 2))
            sp.wait_ge(s_pad[0], 16 * (E // 2 + 1))
            sp.wait_ge(s_pad[1], 16 * (E // 2))

            first_row = sp.alloc_register("first_row")

            def load_tile(j, u):
                sp.reg_load(first_row, table[0:1, 1, bass.ds(j, 1)])
                row = sp.snap(first_row, min_val=0, max_val=E * REGION)
                wait(sp, s_tx, j - 3)
                wait(sp, s_dest, j - 3)
                sp.dma_start(xs[u][:], lists[bass.ds(row, P), :]).then_inc(s_xl[u], 16)

            def next_expert(j):
                first = sp.value_load(table[0:1, 2, bass.ds(j, 1)], min_val=0, max_val=1)
                with sp.If(first == 1):
                    e = sp.value_load(table[0:1, 0, bass.ds(j, 1)], min_val=0, max_val=E - RING)
                    sp.wait_ge(s_dn, j)
                    sp.wait_ge(s_w, 16 * (e + RING - 1))
                    sp.dma_start(ring[:, bass.ds((e + RING - 1) % RING, 1)].squeeze(1).bitcast(F32),
                                 split_w[bass.ds(e + RING - 1, 1)].squeeze(0)).then_inc(s_w, 16)
                with sp.Else():
                    pass

            for j in range(3):
                load_tile(j, j)

            def step_b(j, u, r, in_b):
                ahead = 3
                if isinstance(j, int) and j == 0:
                    sp.wait_ge(s_w, 16 * (RING - 1))
                    sp.dma_start(ring[:, RING - 1].bitcast(F32), split_w[RING - 1]).then_inc(s_w, 16)
                if kind(j, in_b, ahead) == "list":
                    load_tile(j + ahead, (u + ahead) % 4)
                if kind(j, in_b, 0) == "list" and not (isinstance(j, int) and j < 3):
                    next_expert(j - 2)
                if kind(j, in_b, 0) == "shared":
                    if isinstance(j, int) and j == SLOTS:
                        for i in range(4):
                            sp.wait_ge(s_ys[i], 16 * (SLOTS // 4))
                    wait(sp, s_fin, 2 * (j - SLOTS - 3) - 1)
                    sp.dma_start(yr[:, u], routed_t[bass.ds(j - SLOTS, 1)].squeeze(0)).then_inc(s_yl[u], 16)
                if kind(j, in_b, -4) == "shared":
                    sp.wait_ge(s_fin, 2 * (j - SLOTS - 3))
                    sp.dma_start(out[bass.ds(j - SLOTS - 4, 1)].squeeze(0),
                                 X1[:, bass.ds(j - SLOTS - 4, 1)].squeeze(1)).then_inc(s_store, 16)

            each_tile(sp, step_b)
            for t in range(TILES + DRAIN - 4, TILES):
                sp.wait_ge(s_fin, 2 * t + 2)
                sp.dma_start(out[t], X1[:, t]).then_inc(s_store, 16)
            sp.wait_ge(s_store, 16 * TILES)

        @block.gpsimd
        def _(pool):
            def scatter(a, p, r):
                wait_alone(pool, s_pos, POS_STEPS * a + POS_STEPS)
                for j in range(GS):
                    for k in range(TOP):
                        i = TOP * j + k
                        nc.gpsimd.indirect_dma_start(
                            out=lists, out_offset=bass.IndirectOffsetOnAxis(ap=pos[p][:, i:i + 1], axis=0),
                            in_=x2[p][:, j, :], in_offset=None).then_inc(s_scat[p], 16)

            stages(pool, (0, scatter))

            def take_dest(j, u, r):
                wait_alone(pool, s_xl[u], 16 * r + 16)
                wait(pool, s_ys[u], 16 * r)
                e = pool.value_load(table[0:1, 0, bass.ds(j, 1)], min_val=0, max_val=E - 1)
                nc.gpsimd.tensor_copy(dest[u][:], xs[u][:, bass.ds(e + TAG, 1)])
                nc.gpsimd.tensor_copy(gate_j[u][:], xs[u][:, bass.ds(e + GATE, 1)]).then_inc(s_dest, 1)

            def scatter_y(j, u):
                wait_alone(pool, s_y, j + 1)
                pool.wait_ge(s_dest, j + 1)
                nc.gpsimd.indirect_dma_start(
                    out=routed, out_offset=bass.IndirectOffsetOnAxis(ap=dest[u][:, 0:1], axis=0),
                    in_=ysb[u][:], in_offset=None, bounds_check=TOKENS * TOP - 1,
                    oob_is_err=False).then_inc(s_ys[u], 16)

            def add_routed(t, u, r0):
                pool.wait_ge(s_yl[u], 16 * r0 + 16)
                for k in range(1, TOP):
                    if k > 1:
                        pool.wait_ge(s_acc, (TOP - 1) * t + k - 1)
                    nc.gpsimd.tensor_tensor(yr[:, u, 0:D], yr[:, u, 0:D], yr[:, u, k * D:(k + 1) * D],
                                            ALU.add).then_inc(s_acc, 1)

            pool.wait_ge(s_rows, 1)

            def step_b(j, u, r, in_b):
                if kind(j, in_b, -3) == "list":
                    scatter_y(j - 3, (u - 3) % 4)
                if kind(j, in_b, 0) == "list":
                    take_dest(j, u, r)
                if kind(j, in_b, -3) == "shared":
                    add_routed(j - 3 - SLOTS, (u - 3) % 4, r + (u - 3) // 4 - SLOTS // 4)

            each_tile(pool, step_b)

        @block.scalar
        def _(act):
            nc.scalar.preload_act_table_set("natural_log_exp_and_others")
            act.wait_ge(s_const, 16 * CONSTS)

            def split_high(m, p, r):
                act.wait_ge(s_win, 16 * m + 16)
                if isinstance(m, int) and m == 0:
                    nc.scalar.activation(shared[:, 0], wst[:], ACT.Copy).then_inc(s_whi, 1)
                    return
                wait(act, s_wout[p], 16 * r)
                nc.scalar.activation(ring[:, p, 0], wst[:], ACT.Copy).then_inc(s_whi, 1)

            def guess(steps, ln_steps, count, nw, g):
                act.wait_ge(ln_steps, count)
                nc.scalar.activation(nw[:, 1], nw[:, 0], ACT.Ln).then_inc(steps, 1)
                act.wait_ge(steps, 2 * g + 1)
                nc.scalar.activation(nw[:, 2], nw[:, 1], ACT.Exp, scale=-0.5).then_inc(steps, 1)

            def guess1(g, p, r):
                guess(s_ex1, s_ln1, LN1_STEPS * g + 3, nw1, g)

            def guess2(b, p, r):
                guess(s_ex2, s_x1, X1_STEPS * b + 5, nw2, b)

            def exp_logits(a, p, r):
                act.wait_ge(s_lg, a + 1)
                wait(act, s_rt, ROUTE_STEPS * (a - 1) + 1)
                nc.scalar.activation(ez[:].rearrange("p j e -> p (j e)"), p_lg, ACT.Exp, scale=-1.0).then_inc(s_ez, 1)

            def slope(b, p, r):
                act.wait_ge(s_nb, b + 1)
                nc.scalar.activation(att[:].rearrange("p j n -> p (j n)"), p_n[:], ACT.Copy, scale=SLOPE).then_inc(s_slope, 1)

            def exp_scores(b, p, r):
                act.wait_ge(s_att, ATT_STEPS * b + ATT_STEPS)
                wait(act, s_tp, b)
                for j in range(GS):
                    last = nc.scalar.activation(prob[:, j], att[:, j], ACT.Exp, bias=nmax[:, j:j + 1],
                                                accum_out=psums[:, j:j + 1])
                last.then_inc(s_exp, 1)

            def norm1(c, p, r):
                act.wait_ge(s_ln1, LN1_STEPS * c + LN1_STEPS)
                wait(act, s_t1, c - 1)
                for j in range(GS):
                    last = nc.scalar.activation(xn1[:, p, j], X1[:, bass.ds(4 * c + j, 1)].squeeze(1), ACT.Identity,
                                                bias=ln1[:, p, j, 1:2], scale=ln1[:, p, j, 0:1])
                last.then_inc(s_xn1, 1)

            def copy_probT(b, p, r):
                act.wait_ge(s_tp, b + 1)
                wait(act, s_out, b)
                nc.scalar.activation(probT[:].rearrange("p j e -> p (j e)"), p_pt[:], ACT.Copy).then_inc(s_pT, 1)

            def copy_xnT(c, p, r):
                act.wait_ge(s_t1, c + 1)
                wait(act, s_h, c)
                nc.scalar.activation(xnT[:, 0], p_t[0][:], ACT.Copy)
                nc.scalar.activation(xnT[:, 1], p_t[1][:], ACT.Copy).then_inc(s_xnT, 1)

            def copy_h(c, p, r):
                act.wait_ge(s_h, c + 1)
                wait(act, s_out, c - 1)
                wait(act, s_x1, X1_STEPS * (c - 2) + 2)
                for i in range(2):
                    last = nc.scalar.activation(hsb[:, p, 2 * i:2 * i + 2],
                                                p_h[i][:, 0:2 * (O + 2)].rearrange("p (j n) -> p j n", j=2), ACT.Copy)
                last.then_inc(s_hsb, 1)

            def norm2(b, p, r):
                act.wait_ge(s_x1, X1_STEPS * b + X1_STEPS)
                wait(act, s_scat[p], 16 * GROUP_SCATTERS * r)
                for j in range(GS):
                    t = 4 * b + j
                    last = nc.scalar.activation(x2[p][:, j, 0:D], X1[:, bass.ds(t, 1)].squeeze(1), ACT.Identity,
                                                bias=ln2[:, bass.ds(t, 1), 1], scale=ln2[:, bass.ds(t, 1), 0])
                last.then_inc(s_x2, 1)

            def copy_x2T(b, p, r):
                act.wait_ge(s_t2, b + 1)
                wait(act, s_lg, b)
                nc.scalar.activation(x2T[:, 0], p_t[0][:], ACT.Copy)
                nc.scalar.activation(x2T[:, 1], p_t[1][:], ACT.Copy).then_inc(s_x2T, 1)

            def split_next(n, p, r):
                split_high(n + 1, p, r)

            split_high(0, 0, 0)
            stages(act, (2, slope), (3, norm1), (1, guess2), (3, copy_xnT), (2, exp_scores), (3, copy_h), (2, copy_probT),
                   (1, norm2), (1, copy_x2T), (4, guess1), (0, split_next), (1, exp_logits))

            act.wait_ge(s_rows, 1)
            for e in range(1, E, 2):
                c = act.value_load(counts_i[0:1, e:e + 1], min_val=0, max_val=TOKENS)
                act.dma_start(lists[bass.ds(c + e * REGION, P), :], cs[:, C_PAD:C_PAD + ROW]).then_inc(s_pad[1], 16)

            def tile_high(j, u):
                act.wait_ge(s_tx, j + 1)
                nc.scalar.activation(xTh[:, u % 2].rearrange("p k t -> p (k t)"), p_xT[u % 2][:, 0:D],
                                     ACT.Copy).then_inc(s_xh, 1)

            def hidden_high(j, u):
                act.wait_ge(s_th, j + 1)
                nc.scalar.activation(hTh[:, u % 2].rearrange("p k t -> p (k t)"), p_hT[u % 2][:, 0:FF],
                                     ACT.Copy).then_inc(s_hh, 1)

            def silu(j, u):
                act.wait_ge(s_gu, j + 1)
                nc.scalar.activation(gate[:, u % 2], p_gu[u % 2][:, 0:FF], ACT.Silu).then_inc(s_sg, 1)

            def result(j, u, r):
                act.wait_ge(s_dn, j + 1)
                wait(act, s_ys[u], 16 * r)
                act.wait_ge(s_dest, j + 1)
                nc.scalar.activation(ysb[u][:], p_y[u % 2][:, 0:D], ACT.Copy, scale=gate_j[u][:, 0:1]).then_inc(s_y, 1)

            def norm_shared(j, u):
                t = j - SLOTS
                wait(act, s_tx, j - 3)
                if isinstance(j, int) and j < SLOTS + 4:
                    act.wait_ge(s_dest, j - 3)
                nc.scalar.activation(xs[u][:, 0:D], X1[:, bass.ds(t, 1)].squeeze(1), ACT.Identity,
                                     bias=ln2[:, bass.ds(t, 1), 1], scale=ln2[:, bass.ds(t, 1), 0]).then_inc(s_xsh, 1)

            tile_high(0, 0)
            tile_high(1, 1)

            def step_b(j, u, r, in_b):
                if kind(j, in_b, -3) == "list":
                    result(j - 3, (u - 3) % 4, r + (u - 3) // 4)
                if kind(j, in_b, -1):
                    hidden_high(j - 1, (u - 1) % 4)
                if kind(j, in_b, 3) == "shared":
                    norm_shared(j + 3, (u + 3) % 4)
                if kind(j, in_b, 0):
                    silu(j, u)
                if kind(j, in_b, 2):
                    tile_high(j + 2, (u + 2) % 4)

            each_tile(act, step_b)

        @block.vector
        def _(dve):
            dve.wait_ge(s_const, 16 * CONSTS)
            nc.vector.tensor_copy(low_ones[:, 0:P], cs[:, C_LOW:C_LOW + P])
            nc.vector.memset(low_ones[:, P:2 * P], 1.0)
            nc.vector.memset(before[:, 0], 0.0)
            nc.vector.tensor_copy(tagbase[:], cs[:, C_TAG:C_TAG + GS])
            nc.vector.tensor_scalar(mask[:], adj_i[:], -1.0, 1.0, ALU.mult, ALU.add).then_inc(s_prep, 1)
            dve.wait_ge(s_prep, 1)
            nc.vector.tensor_scalar(mask[:], mask[:], NEG, None, ALU.mult).then_inc(s_prep, 1)
            dve.wait_ge(s_wa, 1)
            nc.vector.tensor_copy(wext[:, :, O:O + 2],
                                  p_h[0][:, 0:2 * KD].rearrange("p (k c) -> p k c", k=KD)).then_inc(s_prep, 1)

            def split_low(m, p):
                dve.wait_ge(s_whi, m + 1)
                first = isinstance(m, int) and m == 0
                dst = shared if first else ring[:, p]
                nc.vector.tensor_tensor(dst[:, 1], wst[:], dst[:, 0].bitcast(F32), ALU.subtract).then_inc(s_wlo, 1)

            def attention(b, p, r):
                dve.wait_ge(s_slope, b + 1)
                at0 = ATT_STEPS * b
                pn = p_n[:].rearrange("p (j n) -> p j n", j=GS)
                nc.vector.tensor_tensor(att[:], att[:], pn, ALU.max).then_inc(s_att, 1)
                dve.wait_ge(s_att, at0 + 1)
                nc.vector.tensor_tensor(att[:], att[:], mask[:].unsqueeze(1).to_broadcast([P, GS, P]),
                                        ALU.add).then_inc(s_att, 1)
                dve.wait_ge(s_att, at0 + 2)
                nc.vector.tensor_reduce(nmax[:], att[:], AX_X, ALU.max, negate=True).then_inc(s_att, 1)

            def stats1(c, p, r):
                wait_alone(dve, s_x[p], 16 * r + 16)
                at0 = LN1_STEPS * c
                for j in range(GS):
                    last = nc.vector.bn_stats(st[:, j], X1[:, bass.ds(4 * c + j, 1)].squeeze(1))
                last.then_inc(s_ln1, 1)
                wait_alone(dve, s_ln1, at0 + 1)
                for j in range(GS):
                    last = nc.vector.bn_aggr(mv[:, j], st[:, j])
                last.then_inc(s_ln1, 1)
                dve.wait_ge(s_ln1, at0 + 2)
                nc.vector.tensor_scalar(nw1[:, 0], mv[:, :, 1], EPS, None, ALU.add).then_inc(s_ln1, 1)

            def newton(steps, at0, nw, mean, scale, shift):
                nc.vector.scalar_tensor_tensor(nw[:, 3], nw[:, 0], -0.5, nw[:, 2], ALU.mult, ALU.mult).then_inc(steps, 1)
                dve.wait_ge(steps, at0 + 1)
                nc.vector.tensor_tensor(nw[:, 4], nw[:, 3], nw[:, 2], ALU.mult).then_inc(steps, 1)
                dve.wait_ge(steps, at0 + 2)
                nc.vector.scalar_tensor_tensor(scale, nw[:, 4], 1.5, nw[:, 2], ALU.add, ALU.mult).then_inc(steps, 1)
                dve.wait_ge(steps, at0 + 3)
                nc.vector.scalar_tensor_tensor(shift, mean, -1.0, scale, ALU.mult, ALU.mult).then_inc(steps, 1)

            def newton1(c, p, r):
                dve.wait_ge(s_ex1, 2 * c + 2)
                wait(dve, s_xn1, c - 1)
                newton(s_ln1, LN1_STEPS * c + 3, nw1, mv[:, :, 0], ln1[:, p, :, 0], ln1[:, p, :, 1])

            def add_graph(b, p, r):
                dve.wait_ge(s_out, b + 1)
                at0 = X1_STEPS * b
                nc.vector.reciprocal(rsum[:], psums[:]).then_inc(s_x1, 1)
                dve.wait_ge(s_x1, at0 + 1)
                for j in range(GS):
                    xt = X1[:, bass.ds(4 * b + j, 1), 0:O].squeeze(1)
                    nc.vector.scalar_tensor_tensor(xt, p_o[:, j * O:(j + 1) * O], rsum[:, j:j + 1], xt,
                                                   ALU.mult, ALU.add)
                xh = X1[:, bass.ds(4 * b, GS), O:D]
                nc.vector.tensor_tensor(xh, xh, hsb[:, p, :, 0:O], ALU.add).then_inc(s_x1, 1)
                wait_alone(dve, s_x1, at0 + 2)
                for j in range(GS):
                    last = nc.vector.bn_stats(st2[:, j], X1[:, bass.ds(4 * b + j, 1)].squeeze(1))
                last.then_inc(s_x1, 1)
                wait_alone(dve, s_x1, at0 + 3)
                for j in range(GS):
                    last = nc.vector.bn_aggr(mv2[:, j], st2[:, j])
                last.then_inc(s_x1, 1)
                dve.wait_ge(s_x1, at0 + 4)
                nc.vector.tensor_scalar(nw2[:, 0], mv2[:, :, 1], EPS, None, ALU.add).then_inc(s_x1, 1)

            def newton2(b, p, r):
                dve.wait_ge(s_ex2, 2 * b + 2)
                newton(s_x1, X1_STEPS * b + 5, nw2, mv2[:, :, 0], ln2[:, bass.ds(4 * b, GS), 0],
                       ln2[:, bass.ds(4 * b, GS), 1])

            def route(a, p, r):
                at0 = ROUTE_STEPS * a
                dve.wait_ge(s_ez, a + 1)
                nc.vector.tensor_scalar(aff1[:], ez[:], 1.0, None, ALU.add).then_inc(s_rt, 1)
                dve.wait_ge(s_rt, at0 + 1)
                nc.vector.reciprocal(aff[:], aff1[:]).then_inc(s_rt, 1)
                dve.wait_ge(s_rt, at0 + 2)
                nc.vector.tensor_tensor(score[:], aff[:], bias_s[:].unsqueeze(1).to_broadcast([P, GS, E]),
                                        ALU.add).then_inc(s_rt, 1)
                wait_alone(dve, s_rt, at0 + 3)
                for j in range(GS):
                    last = nc.vector.max(top8[:, j], score[:, j])
                last.then_inc(s_rt, 1)
                wait_alone(dve, s_rt, at0 + 4)
                for j in range(GS):
                    last = nc.vector.max_index(topi[:, j], top8[:, j], score[:, j])
                last.then_inc(s_rt, 1)
                dve.wait_ge(s_rt, at0 + 5)
                nc.vector.tensor_copy(topf[:], topi[:, :, 0:TOP]).then_inc(s_rt, 1)
                dve.wait_ge(s_rt, at0 + 6)
                iota = cs[:, C_IOTA:C_IOTA + E].unsqueeze(1).to_broadcast([P, TOP, E])
                for j in range(GS):
                    last = nc.vector.tensor_tensor(onehot[:, j], topf[:, j].unsqueeze(2).to_broadcast([P, TOP, E]),
                                                   iota, ALU.is_equal)
                last.then_inc(s_rt, 1)
                dve.wait_ge(s_rt, at0 + 7)
                with nc.allow_low_precision("zeros and ones"):
                    nc.vector.tensor_reduce(taken[:], onehot[:].rearrange("p j k e -> p j e k"), AX_X,
                                            ALU.add).then_inc(s_rt, 1)
                dve.wait_ge(s_rt, at0 + 8)
                nc.vector.tensor_tensor(sel[:], taken[:], aff[:], ALU.mult)
                nc.vector.scalar_tensor_tensor(tag1[:], onehot[:, :, 2], 2.0, taken[:], ALU.mult,
                                               ALU.add).then_inc(s_rt, 1)
                dve.wait_ge(s_rt, at0 + 9)
                nc.vector.tensor_tensor(tag2[:], tag1[:], onehot[:, :, 1], ALU.add)
                nc.vector.tensor_reduce(den[:, 0], sel[:], AX_X, ALU.add).then_inc(s_rt, 1)
                dve.wait_ge(s_rt, at0 + 10)
                nc.vector.tensor_tensor(x2[p][:, :, TAG:GATE], tag2[:],
                                        tagbase[:].unsqueeze(2).to_broadcast([P, GS, E]), ALU.add)
                nc.vector.tensor_scalar(den[:, 1], den[:, 0], 1e-9, None, ALU.add).then_inc(s_rt, 1)
                dve.wait_ge(s_rt, at0 + 11)
                nc.vector.tensor_scalar(tagbase[:], tagbase[:], float(TOP * GS * P), None, ALU.add)
                nc.vector.tensor_reduce(newly[:], taken[:].rearrange("p j e -> p e j"), AX_X, ALU.add)
                nc.vector.reciprocal(den[:, 2], den[:, 1]).then_inc(s_rt, 1)
                dve.wait_ge(s_rt, at0 + 12)
                with nc.allow_low_precision("whole numbers up to 64"):
                    nc.vector.tensor_tensor(before[:, 1 - p], before[:, p], newly[:], ALU.add)
                nc.vector.tensor_tensor(x2[p][:, :, GATE:ROW], aff[:], den[:, 2].unsqueeze(2).to_broadcast([P, GS, E]),
                                        ALU.mult).then_inc(s_rt, 1)

            def positions(a, p, r):
                at0 = POS_STEPS * a
                dve.wait_ge(s_rk, a + 1)
                nc.vector.tensor_tensor(rankb[:], p_rk.rearrange("p (j e) -> p j e", j=GS),
                                        cs[:, C_BASE:C_BASE + E].unsqueeze(1).to_broadcast([P, GS, E]),
                                        ALU.add).then_inc(s_pos, 1)
                dve.wait_ge(s_pos, at0 + 1)
                for j in range(GS):
                    last = nc.vector.tensor_tensor(selpos[:, j], onehot[:, j],
                                                   rankb[:, j].unsqueeze(1).to_broadcast([P, TOP, E]), ALU.mult)
                last.then_inc(s_pos, 1)
                dve.wait_ge(s_pos, at0 + 2)
                nc.vector.tensor_reduce(posf[:], selpos[:], AX_X, ALU.add).then_inc(s_pos, 1)
                dve.wait_ge(s_pos, at0 + 3)
                nc.vector.tensor_copy(pos[p][:], posf[:].rearrange("p j k -> p (j k)")).then_inc(s_pos, 1)

            def split_next(n, p, r):
                split_low(n + 1, p)

            split_low(0, 0)
            stages(dve, (1, add_graph), (2, attention), (0, route), (1, newton2), (4, stats1),
                   (0, positions), (0, split_next), (4, newton1))

            dve.wait_ge(s_cnt, 1)
            nc.vector.tensor_copy(cnt[:], bank[7][:, 0:E]).then_inc(s_tb, 1)
            dve.wait_ge(s_tb, 1)
            nc.vector.tensor_scalar(ntf[:], cnt[:], 1.0 / P, (P - 1) / 2 / P, ALU.mult, ALU.add).then_inc(s_tb, 1)
            nc.vector.tensor_copy(counts_i[:], cnt[0:1, :])
            dve.wait_ge(s_tb, 2)
            nc.vector.tensor_copy(nti[:], ntf[:]).then_inc(s_tb, 1)
            dve.wait_ge(s_tb, 3)
            nc.vector.tensor_scalar(ntf[:], nti[:], 1.0, None, ALU.max).then_inc(s_tb, 1)
            dve.wait_ge(s_tb, 4)
            nc.vector.tensor_tensor_scan(cum[:], cs[:, C_ONE:C_ONE + E], ntf[:], 0.0, ALU.mult, ALU.add)\
                .then_inc(s_tb, 1)
            dve.wait_ge(s_tb, 5)
            jt = cs[:, C_TILE:C_TILE + 2]
            nc.vector.tensor_tensor(ended[:], cum[:].unsqueeze(1).to_broadcast([P, 2, E]),
                                    jt.unsqueeze(2).to_broadcast([P, 2, E]), ALU.is_le).then_inc(s_tb, 1)
            dve.wait_ge(s_tb, 6)
            nc.vector.tensor_tensor(tmp3[:], ended[:], cs[:, C_MOVE:C_MOVE + E].unsqueeze(1).to_broadcast([P, 2, E]),
                                    ALU.mult)
            nc.vector.tensor_reduce(ej[:, 0], ended[:], AX_X, ALU.add)
            nc.vector.tensor_tensor(tmp2[:], ended[:], ntf[:].unsqueeze(1).to_broadcast([P, 2, E]),
                                    ALU.mult).then_inc(s_tb, 1)
            dve.wait_ge(s_tb, 7)
            nc.vector.tensor_reduce(tv[:, 3], tmp3[:], AX_X, ALU.add)
            nc.vector.tensor_reduce(ej[:, 1], tmp2[:], AX_X, ALU.add).then_inc(s_tb, 1)
            dve.wait_ge(s_tb, 8)
            nc.vector.tensor_tensor(ej[:, 2], jt, ej[:, 1], ALU.subtract)
            nc.vector.tensor_tensor(ej[:, 3], jt, ej[:, 1], ALU.is_equal)
            nc.vector.tensor_scalar(ej[:, 4], ej[:, 0], float(REGION), None, ALU.mult)
            nc.vector.tensor_scalar(ej[:, 6], ej[:, 0], float(E - RING), None, ALU.is_le)
            nc.vector.tensor_scalar(tv[:, 0], ej[:, 0], float(E - 1), None, ALU.min).then_inc(s_tb, 1)
            dve.wait_ge(s_tb, 9)
            nc.vector.scalar_tensor_tensor(ej[:, 5], ej[:, 2], float(P), ej[:, 4], ALU.mult, ALU.add)
            nc.vector.tensor_tensor(tv[:, 2], ej[:, 3], ej[:, 6], ALU.mult).then_inc(s_tb, 1)
            dve.wait_ge(s_tb, 10)
            nc.vector.tensor_scalar(tv[:, 1], ej[:, 5], float(E * REGION), None, ALU.min).then_inc(s_tb, 1)
            dve.wait_ge(s_tb, 12)
            nc.vector.tensor_copy(table[:, 0:2].rearrange("p v j -> p (v j)"), bank[6][0:1, :])
            nc.vector.tensor_copy(table[:, 2:4].rearrange("p v j -> p (v j)"), bank[5][0:1, :]).then_inc(s_rows, 1)

            def weights_in(j):
                e = dve.value_load(table[0:1, 0, bass.ds(j, 1)], min_val=0, max_val=E - 1)
                dve.wait_ge(s_w, 16 * (e + 1))

            def tile_low(j, u):
                dve.wait_ge(s_xh, j + 1)
                nc.vector.tensor_tensor(xTl[:, u % 2].rearrange("p k t -> p (k t)"), p_xT[u % 2][:, 0:D],
                                        xTh[:, u % 2].rearrange("p k t -> p (k t)").bitcast(F32),
                                        ALU.subtract).then_inc(s_xlo, 1)

            def hidden_low(j, u):
                dve.wait_ge(s_hh, j + 1)
                nc.vector.tensor_tensor(hTl[:, u % 2].rearrange("p k t -> p (k t)"), p_hT[u % 2][:, 0:FF],
                                        hTh[:, u % 2].rearrange("p k t -> p (k t)").bitcast(F32),
                                        ALU.subtract).then_inc(s_hl, 1)

            def multiply(j, u):
                dve.wait_ge(s_sg, j + 1)
                nc.vector.tensor_tensor(hid[:, u % 2], p_gu[u % 2][:, FF:WIDE], gate[:, u % 2],
                                        ALU.mult).then_inc(s_hid, 1)

            def finish(j, u):
                t = j - SLOTS
                xt = X1[:, bass.ds(t, 1)].squeeze(1)
                dve.wait_ge(s_acc, (TOP - 1) * (t + 1))
                dve.wait_ge(s_xsh, t + 1)
                nc.vector.tensor_tensor(xt, yr[:, u, 0:D], xt, ALU.add).then_inc(s_fin, 1)
                dve.wait_ge(s_fin, 2 * t + 1)
                dve.wait_ge(s_dn, j + 1)
                nc.vector.tensor_tensor(xt, p_y[u % 2][:, 0:D], xt, ALU.add).then_inc(s_fin, 1)

            dve.wait_ge(s_rows, 1)
            weights_in(0)
            tile_low(0, 0)
            weights_in(1)
            tile_low(1, 1)

            def step_b(j, u, r, in_b):
                if kind(j, in_b, -3) == "shared":
                    finish(j - 3, (u - 3) % 4)
                if kind(j, in_b, -1):
                    hidden_low(j - 1, (u - 1) % 4)
                if kind(j, in_b, 0):
                    multiply(j, u)
                if kind(j, in_b, 2) == "list":
                    weights_in(j + 2)
                if kind(j, in_b, 2):
                    tile_low(j + 2, (u + 2) % 4)

            each_tile(dve, step_b)

        @block.tensor
        def _(pe):
            pe.wait_ge(s_const, 16 * CONSTS)
            for k in range(KD):
                last = nc.tensor.matmul(p_h[0][:, 2 * k:2 * k + 2], wts[:, k * P:(k + 1) * P], ats[:],
                                        start=True, stop=True)
            last.then_inc(s_wa, 1)
            pe.wait_ge(s_prep, 3)

            def score_sums(b, p, r):
                pe.wait_ge(s_hsb, b + 1)
                wait(pe, s_pT, b)
                for j in range(GS):
                    dst = p_n[:, j * P:(j + 1) * P]
                    nc.tensor.matmul(dst, hsb[:, p, j, O + 1:O + 2].to_broadcast([P, P]), ident, start=True, stop=False)
                    last = nc.tensor.matmul(dst, ident, hsb[:, p, j, O:O + 1].to_broadcast([P, P]),
                                            start=False, stop=True)
                last.then_inc(s_nb, 1)

            def transpose_prob(b, p, r):
                pe.wait_ge(s_exp, b + 1)
                for j in range(GS):
                    last = nc.tensor.transpose(p_pt[:, j * P:(j + 1) * P], prob[:, j], ident)
                last.then_inc(s_tp, 1)

            def transpose_xn1(c, p, r):
                pe.wait_ge(s_xn1, c + 1)
                wait(pe, s_x2T, c - 2)
                wait(pe, s_xnT, c)
                for k in range(KD):
                    for j in range(GS):
                        last = nc.tensor.transpose(p_t[k][:, j * P:(j + 1) * P], xn1[:, p, j, k * P:(k + 1) * P], ident)
                last.then_inc(s_t1, 1)

            def attend(b, p, r):
                pe.wait_ge(s_pT, b + 1)
                wait(pe, s_x1, X1_STEPS * (b - 1) + 2)
                for j in range(GS):
                    last = nc.tensor.matmul(p_o[:, j * O:(j + 1) * O], probT[:, j], hsb[:, p, j, 0:O],
                                            start=True, stop=True)
                last.then_inc(s_out, 1)

            def ranks(a, p, r):
                pe.wait_ge(s_rt, ROUTE_STEPS * a + 8)
                nc.tensor.matmul(p_rk, lower, taken[:].rearrange("p j e -> p (j e)"), start=True, stop=False)
                for j in range(GS - 1):
                    n = GS - 1 - j
                    nc.tensor.matmul(p_rk[:, (j + 1) * E:].rearrange("p (j e) -> p j e", j=n), ones,
                                     taken[:, j:j + 1].to_broadcast([P, n, E]), start=False, stop=False)
                nc.tensor.matmul(p_rk.rearrange("p (j e) -> p j e", j=GS), ones,
                                 before[:, p:p + 1].to_broadcast([P, GS, E]), start=False, stop=True).then_inc(s_rk, 1)

            def project(c, p, r):
                pe.wait_ge(s_xnT, c + 1)
                wait(pe, s_hsb, c)
                for j in range(GS):
                    for k in range(KD):
                        last = nc.tensor.matmul(p_h[j // 2][:, (j % 2) * (O + 2):(j % 2 + 1) * (O + 2)],
                                                xnT[:, k, j * P:(j + 1) * P], wext[:, k],
                                                start=(k == 0), stop=(k == KD - 1))
                last.then_inc(s_h, 1)

            def transpose_x2(b, p, r):
                pe.wait_ge(s_x2, b + 1)
                for k in range(KD):
                    for j in range(GS):
                        last = nc.tensor.transpose(p_t[k][:, j * P:(j + 1) * P], x2[p][:, j, k * P:(k + 1) * P], ident)
                last.then_inc(s_t2, 1)

            def logits(b, p, r):
                pe.wait_ge(s_x2T, b + 1)
                wait(pe, s_ez, b)
                for j in range(GS):
                    for k in range(KD):
                        last = nc.tensor.matmul(p_lg[:, j * E:(j + 1) * E], x2T[:, k, j * P:(j + 1) * P], gws[:, k],
                                                start=(k == 0), stop=(k == KD - 1))
                last.then_inc(s_lg, 1)

            stages(pe, (2, score_sums), (3, transpose_xn1), (3, project), (2, transpose_prob),
                   (0, ranks), (2, attend), (1, transpose_x2), (1, logits))

            pe.wait_ge(s_rt, ROUTE_STEPS * GROUPS)
            pe.wait_ge(s_pos, POS_STEPS * GROUPS)
            nc.tensor.matmul(bank[7][:, 0:E], ones, before[:, GROUPS % 2], start=True, stop=True).then_inc(s_cnt, 1)
            pe.wait_ge(s_tb, 11)
            for v in range(4):
                for h in range(2):
                    at0 = (v % 2) * 2 * P + h * P
                    last = nc.tensor.matmul(bank[6 - v // 2][0:1, at0:at0 + P], tv[:, v, h:h + 1], ident,
                                            start=True, stop=True)
            last.then_inc(s_tb, 1)
            pe.wait_ge(s_rows, 1)

            def transpose_tile(j, u, r, what):
                if what == "list":
                    pe.wait_ge(s_xl[u], 16 * r + 16)
                else:
                    pe.wait_ge(s_xsh, j - SLOTS + 1)
                for k in range(KD):
                    last = nc.tensor.transpose(p_xT[u % 2][:, k * P:(k + 1) * P], xs[u][:, k * P:(k + 1) * P], ident)
                last.then_inc(s_tx, 1)

            ring_w = ring[:].rearrange("p r h c -> p (r h c)")
            places = [pe.alloc_register(f"place{i}") for i in range(4)]

            def load_place(j, u):
                pe.reg_load(places[u], table[0:1, 3, bass.ds(j, 1)])

            def product(dst, xh, xl, u, what, at0, width, first, last_one):
                if what == "shared":
                    wh, wl = (shared[:, h, at0:at0 + width] for h in range(2))
                else:
                    place = pe.snap(places[u], min_val=0, max_val=(RING - 1) * 2 * WX)
                    wh, wl = (ring_w[:, bass.ds(place + (h * WX + at0), width)] for h in range(2))
                nc.tensor.matmul(dst, xh, wh, start=first, stop=False)
                nc.tensor.matmul(dst, xl, wh, start=False, stop=False)
                return nc.tensor.matmul(dst, xh, wl, start=False, stop=last_one)

            def gate_up(j, u, what, k):
                if k == 0:
                    pe.wait_ge(s_xlo, j + 1)
                last = product(p_gu[u % 2][:, 0:WIDE], xTh[:, u % 2, k], xTl[:, u % 2, k], u, what, k * WIDE, WIDE,
                               k == 0, k == KD - 1)
                if k == KD - 1:
                    last.then_inc(s_gu, 1)

            def transpose_hidden(j, u):
                pe.wait_ge(s_hid, j + 1)
                for k in range(KF):
                    last = nc.tensor.transpose(p_hT[u % 2][:, k * P:(k + 1) * P], hid[:, u % 2, k * P:(k + 1) * P], ident)
                last.then_inc(s_th, 1)

            def down(j, u, what):
                pe.wait_ge(s_hl, j + 1)
                for k in range(KF):
                    last = product(p_y[u % 2][:, 0:D], hTh[:, u % 2, k], hTl[:, u % 2, k], u, what,
                                   KD * WIDE + k * D, D, k == 0, k == KF - 1)
                last.then_inc(s_dn, 1)

            load_place(0, 0)
            transpose_tile(0, 0, 0, "list")
            transpose_tile(1, 1, 0, "list")

            def step_b(j, u, r, in_b):
                what = kind(j, in_b, 0)
                if what:
                    gate_up(j, u, what, 0)
                    gate_up(j, u, what, 1)
                if kind(j, in_b, -1):
                    transpose_hidden(j - 1, (u - 1) % 4)
                if kind(j, in_b, -2):
                    down(j - 2, (u - 2) % 4, kind(j, in_b, -2))
                if kind(j, in_b, 2):
                    transpose_tile(j + 2, (u + 2) % 4, r + (u + 2) // 4, kind(j, in_b, 2))
                if kind(j, in_b, 1) == "list":
                    load_place(j + 1, (u + 1) % 4)

            each_tile(pe, step_b)


def kernel(x, adj, L0_gnn_W, L0_gnn_a, L0_ffn_gate_w, L0_ffn_expert_bias, L0_ffn_shared_gate_up,
           L0_ffn_shared_down, L0_ffn_expert_gate_up, L0_ffn_expert_down):
    import numpy as np
    import concourse.bacc as bacc
    from concourse.bass_utils import run_bass_kernel_spmd

    def chunks(a):
        n, kp, m = a.shape
        return a.reshape(n, kp // P, P, m).transpose(0, 2, 1, 3).reshape(n, P, -1)

    gate_up = np.concatenate([np.asarray(L0_ffn_shared_gate_up)[None], np.asarray(L0_ffn_expert_gate_up)])
    down = np.concatenate([np.asarray(L0_ffn_shared_down)[None], np.asarray(L0_ffn_expert_down)])
    weights = np.concatenate([chunks(gate_up.transpose(0, 2, 1)), chunks(down.transpose(0, 2, 1))], axis=2)
    w = np.asarray(L0_gnn_W)
    arrays = {
        "x": np.asarray(x),
        "adj": np.asarray(adj),
        "w": chunks(w[None])[0].reshape(P, KD, O),
        "wt": w.T,
        "at": np.asarray(L0_gnn_a)[:, :, 0].T,
        "gate_wt": chunks(np.asarray(L0_ffn_gate_w).T[None])[0].reshape(P, KD, E),
        "bias": np.broadcast_to(np.asarray(L0_ffn_expert_bias), (P, E)),
        "weights": weights,
        "consts": constants(),
    }
    arrays = {f"in_{k}": np.ascontiguousarray(v) for k, v in arrays.items()}
    nc = bacc.Bacc("TRN2", target_bir_lowering=False, num_devices=1)
    aps = [nc.dram_tensor(k, v.shape, mybir.dt.from_np(v.dtype), kind="ExternalInput").ap() for k, v in arrays.items()]
    out = nc.dram_tensor("out_0", (TILES, P, D), F32, kind="ExternalOutput").ap()
    build(nc, *aps, out)
    r = run_bass_kernel_spmd(nc, [arrays], core_ids=[0])
    return r.results[0]["out_0"]
```

```python
import math
from contextlib import ExitStack

import concourse.bass as bass
from concourse import mybir

ALU = mybir.AluOpType
ACT = mybir.ActivationFunctionType
AX_X = mybir.AxisListType.X
F32 = mybir.dt.float32
F32R = mybir.dt.float32r
BF16 = mybir.dt.bfloat16
I32 = mybir.dt.int32
U32 = mybir.dt.uint32

P = 128
TILES = 64
TOKENS = TILES * P
D = 256
KD = D // P
O = 128
FF = 256
KF = FF // P
E = 16
TOP = 3
EPS = 1e-5
SLOPE = 0.2
NEG = -1e9

GS = 4
GROUPS = TILES // GS

REGION = TOKENS + P
TAG, GATE = D, D + E
ROW = D + 2 * E
LIST_ROWS = E * REGION + P
NO_ROW = 4 * TOKENS * TOP

SLOTS = (TOKENS * TOP + E * (P - 1)) // P
SLOTS += -SLOTS % 8
WIDE = 2 * FF
WX = KD * WIDE + KF * D
RING = 8
EARLY = 4

C_ID, C_LOW = 0, P
C_IOTA = 2 * P
C_BASE = C_IOTA + E
C_TAG = C_BASE + E
C_TILE = C_TAG + GS
C_PAD = C_TILE + 2
C_ONE = C_PAD + ROW
C_MOVE = C_ONE + E
C_ALL = C_MOVE + E

GROUP_SCATTERS = GS * TOP


def constants():
    import numpy as np

    c = np.zeros((P, C_ALL), np.float32)
    p = np.arange(P)
    c[:, C_ID:C_ID + P] = np.eye(P)
    c[:, C_LOW:C_LOW + P] = p[:, None] < p[None, :]
    c[:, C_IOTA:C_IOTA + E] = np.arange(E)
    c[:, C_BASE:C_BASE + E] = np.arange(E) * REGION
    c[:, C_TAG:C_TAG + GS] = TOP * (P * np.arange(GS)[None, :] + p[:, None]) - 1
    c[:, C_TILE:C_TILE + 2] = P * np.arange(2)[None, :] + p[:, None]
    c[:, C_PAD + TAG:C_PAD + GATE] = NO_ROW
    c[:, C_ONE:C_ONE + E] = 1.0
    place = 2 * WX * (np.arange(E + 1) % RING)
    c[:, C_MOVE:C_MOVE + E] = place[1:] - place[:-1]
    return c


def build(nc, x, adj, w, wt, at, gate_wt, bias, weights, consts, out):
    with ExitStack() as ctx:
        def sb(name, shape, dt):
            return ctx.enter_context(nc.sbuf_tensor(name, shape, dt))

        def sem(name):
            return ctx.enter_context(nc.semaphore(name))

        def wait(eng, s, value):
            if isinstance(value, Group):
                value = value + 0
            if not (isinstance(value, int) and value <= 0):
                eng.wait_ge(s, value)

        def wait_alone(eng, s, value):
            value = value if isinstance(value, int) else eng.to_reg(value)
            eng.wait_ge(s_const, 16 * CONSTS)
            eng.wait_ge(s, value)

        lists = nc.dram_tensor("lists", [LIST_ROWS, ROW], F32).ap()
        split_w = nc.dram_tensor("split_w", [E, P, 2, WX], F32).ap()
        routed = nc.dram_tensor("routed", [TOKENS * TOP, D], F32).ap()
        routed_t = routed.rearrange("(t p k) d -> t p (k d)", p=P, k=TOP)

        X1 = sb("X1", [P, TILES, D], F32)
        ln2 = sb("ln2", [P, TILES, 2], F32)
        cs = sb("cs", [P, C_ALL], F32)
        ident = cs[:, C_ID:C_ID + P]
        ring = sb("ring", [P, RING, 2, WX], F32R)
        shared = sb("shared", [P, 2, WX], F32R)
        table = sb("table", [1, 4, 2 * P], I32)
        counts_i = sb("counts_i", [1, E], I32)

        wext = sb("wext", [P, KD, O + 2], F32)
        ats = sb("ats", [P, 2], F32)
        gws = sb("gws", [P, KD, E], F32)
        bias_s = sb("bias_s", [P, E], F32)
        adj_i = sb("adj_i", [P, P], I32)
        mask = sb("mask", [P, P], F32)
        low_ones = sb("low_ones", [P, 2 * P], BF16)
        lower, ones = low_ones[:, 0:P], low_ones[:, P:2 * P]
        st = sb("st", [P, GS, 6], F32)
        mv = sb("mv", [P, GS, 2], F32)
        nw1 = sb("nw1", [P, 5, GS], F32)
        ln1 = sb("ln1", [P, 2, GS, 2], F32)
        st2 = sb("st2", [P, GS, 6], F32)
        mv2 = sb("mv2", [P, GS, 2], F32)
        nw2 = sb("nw2", [P, 5, GS], F32)
        nmax = sb("nmax", [P, GS], F32)
        psums = sb("psums", [P, GS], F32)
        rsum = sb("rsum", [P, GS], F32)
        tagbase = sb("tagbase", [P, GS], F32)
        ez = sb("ez", [P, GS, E], F32)
        aff1 = sb("aff1", [P, GS, E], F32)
        aff = sb("aff", [P, GS, E], F32)
        score = sb("score", [P, GS, E], F32)
        top8 = sb("top8", [P, GS, 8], F32)
        topi = sb("topi", [P, GS, 8], U32)
        topf = sb("topf", [P, GS, TOP], F32)
        taken = sb("taken", [P, GS, E], BF16)
        tag1 = sb("tag1", [P, GS, E], F32)
        tag2 = sb("tag2", [P, GS, E], F32)
        sel = sb("sel", [P, GS, E], F32)
        den = sb("den", [P, 3, GS], F32)
        before = sb("before", [P, 2, E], BF16)
        newly = sb("newly", [P, E], F32)
        rankb = sb("rankb", [P, GS, E], F32)
        posf = sb("posf", [P, GS, TOP], F32)
        pos = [sb(f"pos_{i}", [P, GS * TOP], I32) for i in range(2)]

        def in_slot(slot, at0, *shape):
            size = math.prod(shape)
            assert at0 + size <= 2 * WX
            flat = ring[:, EARLY + slot].rearrange("p h c -> p (h c)").bitcast(F32)[:, at0:at0 + size]
            names = "abc"[:len(shape)]
            return flat.rearrange("p (%s) -> p %s" % (" ".join(names), " ".join(names)), **dict(zip(names, shape)))

        xn1 = in_slot(0, 0, 2 * GS, D).rearrange("p (i j) d -> p i j d", i=2)
        xnT = in_slot(0, 2 * GS * D, KD, GS * P)
        att = in_slot(1, 0, GS, P)
        prob = in_slot(1, GS * P, GS, P)
        probT = in_slot(1, 2 * GS * P, GS, P)
        x2T = in_slot(1, 3 * GS * P, KD, GS * P)
        wts = in_slot(1, (3 + KD) * GS * P, D)
        wst = in_slot(2, 0, WX)
        hsb = in_slot(2, WX, 2 * GS, O + 2).rearrange("p (i j) d -> p i j d", i=2)
        x2 = [in_slot(3, i * GS * ROW, GS, ROW) for i in range(2)]
        onehot, selpos = (in_slot(3, 2 * GS * ROW + i * GS * TOP * E, GS * TOP, E)
                          .rearrange("p (j k) e -> p j k e", j=GS) for i in range(2))

        cnt = sb("cnt", [P, E], F32)
        nti = sb("nti", [P, E], I32)
        ntf = sb("ntf", [P, E], F32)
        cum = sb("cum", [P, E], F32)
        ended = sb("ended", [P, 2, E], F32)
        tmp2 = sb("tmp2", [P, 2, E], F32)
        ej = sb("ej", [P, 8, 2], F32)
        tv = sb("tv", [P, 4, 2], F32)
        tmp3 = sb("tmp3", [P, 2, E], F32)

        xs = [sb(f"xs_{i}", [P, ROW], F32) for i in range(4)]
        gate_j = [sb(f"gate_j_{i}", [P, 1], F32) for i in range(8)]
        dest = [sb(f"dest_{i}", [P, 1], I32) for i in range(8)]
        xTh = sb("xTh", [P, 2, KD, P], F32R)
        xTl = sb("xTl", [P, 2, KD, P], F32R)
        gate = sb("gate", [P, 2, FF], F32)
        hid = sb("hid", [P, 2, FF], F32)
        hTh = sb("hTh", [P, 2, KF, P], F32R)
        hTl = sb("hTl", [P, 2, KF, P], F32R)
        ysb = [sb(f"ysb_{i}", [P, D], F32) for i in range(4)]
        yr = ring[:, 0].rearrange("p h c -> p (h c)").bitcast(F32).rearrange("p (u c) -> p u c", u=4)

        bank = [ctx.enter_context(nc.psum_tensor(f"bank{i}", [P, 512], F32)) for i in range(8)]
        p_t = bank[0:2]
        p_h = bank[2:4]
        p_n, p_pt, p_o = bank[4], bank[4], bank[6]
        p_lg = bank[7][:, 0:GS * E]
        p_rk = bank[5][:, 0:GS * E]
        p_xT, p_gu, p_hT, p_y = bank[0:2], bank[2:4], bank[4:6], bank[6:8]

        s_const = sem("const_loaded")
        s_x = [sem(f"x_loaded{i}") for i in range(2)]
        s_wa = sem("wa_product")
        s_prep = sem("vector_prepared")
        s_win = sem("weights_in")
        s_whi = sem("weights_high")
        s_wlo = sem("weights_low")
        s_wout = [sem(f"weights_out{i}") for i in range(2)]
        s_ln1 = [sem(f"ln1_step{i}") for i in range(7)]
        s_ex1 = [sem(f"guess1_step{i}") for i in range(2)]
        s_ex2 = [sem(f"guess2_step{i}") for i in range(2)]
        s_xn1 = sem("xn1_ready")
        s_t1 = sem("xn1_transposed")
        s_xnT = sem("xnT_ready")
        s_h = sem("h_product")
        s_hsb = sem("h_ready")
        s_nb = sem("neighbour_rows")
        s_slope = sem("scores_sloped")
        s_att = [sem(f"attention_step{i}") for i in range(3)]
        s_exp = sem("prob_ready")
        s_tp = sem("prob_transposed")
        s_pT = sem("probT_ready")
        s_out = sem("attended")
        s_xh1 = sem("x1_h_added")
        s_x1 = [sem(f"x1_step{i}") for i in range(9)]
        s_x2 = sem("x2_ready")
        s_t2 = sem("x2_transposed")
        s_x2T = sem("x2T_ready")
        s_lg = sem("logits")
        s_ez = sem("exp_logits")
        s_rt = [sem(f"route_step{i}") for i in range(13)]
        s_rk = sem("ranks")
        s_pos = [sem(f"position_step{i}") for i in range(4)]
        s_scat = [sem(f"scattered{i}") for i in range(2)]
        s_cnt = sem("counts")
        s_tb = sem("table_steps")
        s_rows = sem("table_rows")
        s_pad_spare = sem("padded_spare")
        s_pad = [sem(f"padded_{i}") for i in ("sp", "act")]
        s_xl = [sem(f"list_tile_loaded{i}") for i in range(4)]
        s_w = sem("expert_weights_loaded")
        s_xsh = sem("shared_tile_ready")
        s_tx = sem("tile_transposed")
        s_xh = sem("tile_high")
        s_xlo = sem("tile_low")
        s_gu = sem("gate_up")
        s_sg = sem("gate_ready")
        s_hid = sem("hidden_ready")
        s_th = sem("hidden_transposed")
        s_hh = sem("hidden_high")
        s_hl = sem("hidden_low")
        s_dn = sem("down")
        s_y = sem("result_ready")
        s_dest = sem("dest_ready")
        s_ys = [sem(f"result_scattered{i}") for i in range(4)]
        s_yl = [sem(f"routed_loaded{i}") for i in range(4)]
        s_acc = sem("routed_added")
        s_fin = sem("tile_finished")
        s_store = sem("stored")

        CONSTS = 7
        xg = x.rearrange("(g j) p d -> g p j d", j=GS)

        class Group:
            def __init__(self, eng, twice, k, sums):
                self.eng, self.twice, self.k, self.sums = eng, twice, k, sums

            def at(self, k):
                return Group(self.eng, self.twice, self.k + k, self.sums)

            def __add__(self, k):
                if self.k + k not in self.sums:
                    self.sums[self.k + k] = self.eng.snap(self.twice + (self.k + k), min_val=2 + self.k + k,
                                                             max_val=GROUPS + self.k + k)
                return self.sums[self.k + k]

            def __sub__(self, k):
                return self + -k

            def __rmul__(self, times):
                return times * self.twice + times * self.k

        def later(n, k):
            return n + k if isinstance(n, int) else n.at(k)

        def each_group(eng, body):
            for n in range(-4, 2):
                body(n, n % 2, n // 2)
            with eng.Fori(1, (GROUPS - 4) // 2) as i:
                sums = {}
                body(Group(eng, 2 * i, 0, sums), 0, i)
                body(Group(eng, 2 * i, 1, sums), 1, i)
            for n in range(GROUPS - 4, GROUPS):
                body(n, n % 2, n // 2)

        def ahead(n, p, r, lag):
            if isinstance(n, int) and not 0 <= n + lag < GROUPS:
                return None
            return later(n, lag), (p + lag) % 2, r + (p + lag) // 2

        def stages(eng, *parts):
            def step(n, p, r):
                for lag, part in parts:
                    g = ahead(n, p, r, lag)
                    if g is not None:
                        part(*g)
            each_group(eng, step)

        DRAIN = 3

        def each_tile(eng, body):
            total = SLOTS + TILES
            for j in range(0, 8):
                body(j, j % 8, j // 4, True)
            with eng.Fori(1, SLOTS // 8 - 1) as i:
                for u in range(8):
                    body(8 * i + u, u, 2 * i + u // 4, True)
            for j in range(SLOTS - 8, SLOTS + 8):
                body(j, j % 8, j // 4, j < SLOTS)
            with eng.Fori(SLOTS // 8 + 1, total // 8 - 1) as i:
                for u in range(8):
                    body(8 * i + u, u, 2 * i + u // 4, False)
            for j in range(total - 8, total + DRAIN):
                body(j, j % 8, j // 4, False)

        def kind(j, in_b, lag):
            if not isinstance(j, int):
                return "list" if in_b else "shared"
            return "list" if 0 <= j + lag < SLOTS else "shared" if SLOTS <= j + lag < SLOTS + TILES else None

        pad = cs[:, C_PAD:C_PAD + ROW]

        def pad_list(eng, e, padded):
            c = eng.value_load(counts_i[0:1, e:e + 1], min_val=0, max_val=TOKENS)
            eng.dma_start(lists[bass.ds(c + e * REGION, P), :], pad).then_inc(padded, 16)

        block = ctx.enter_context(nc.Block())

        @block.sync
        def _(sp):
            for dst, src in ((cs[:], consts), (wts[:], wt), (ats[:], at), (gws[:], gate_wt), (bias_s[:], bias),
                             (adj_i[:], adj), (wext[:, :, 0:O], w)):
                sp.dma_start(dst, src).then_inc(s_const, 16)

            def load_weights(m):
                wait(sp, s_wlo, m)
                sp.dma_start(wst[:], weights[bass.ds(m + 0, 1)].squeeze(0)).then_inc(s_win, 16)

            def store_weights(e, p, r):
                sp.wait_ge(s_whi, e + 2)
                sp.wait_ge(s_wlo, e + 2)
                sp.dma_start(split_w[bass.ds(e + 0, 1)].squeeze(0), ring[:, p].bitcast(F32)).then_inc(s_wout[p], 16)

            load_weights(0)

            def expert_weights(e, p, r):
                load_weights(later(e, 1))
                store_weights(e, p, r)

            stages(sp, (3, expert_weights))

            sp.wait_ge(s_wout[0], 16 * (E // 2))
            sp.wait_ge(s_wout[1], 16 * (E // 2))
            for e in range(EARLY):
                wait(sp, s_w, 16 * e)
                sp.dma_start(ring[:, e].bitcast(F32), split_w[e]).then_inc(s_w, 16)

            sp.wait_ge(s_const, 16 * CONSTS)
            sp.dma_start(lists[E * REGION:E * REGION + P, :], pad).then_inc(s_pad_spare, 16)
            sp.wait_ge(s_rows, 1)
            for e in range(0, E, 2):
                pad_list(sp, e, s_pad[0])
            sp.wait_ge(s_scat[0], 16 * GROUP_SCATTERS * (GROUPS // 2))
            sp.wait_ge(s_scat[1], 16 * GROUP_SCATTERS * (GROUPS // 2))
            sp.wait_ge(s_pad[0], 16 * (E // 2))
            sp.wait_ge(s_pad[1], 16 * (E // 2))
            sp.wait_ge(s_pad_spare, 16)

            first_row = sp.alloc_register("first_row")

            def load_tile(j, u):
                sp.reg_load(first_row, table[0:1, 1, bass.ds(j, 1)])
                row = sp.snap(first_row, min_val=0, max_val=E * REGION)
                wait(sp, s_tx, j - 3)
                wait(sp, s_dest, j - 3)
                sp.dma_start(xs[u % 4][:], lists[bass.ds(row, P), :]).then_inc(s_xl[u % 4], 16)

            def next_expert(j):
                first = sp.value_load(table[0:1, 2, bass.ds(j, 1)], min_val=0, max_val=1)
                with sp.If(first == 1):
                    e = sp.value_load(table[0:1, 0, bass.ds(j, 1)], min_val=0, max_val=E - RING)
                    sp.wait_ge(s_dn, j)
                    sp.wait_ge(s_w, 16 * (e + RING - 1))
                    sp.dma_start(ring[:, bass.ds((e + RING - 1) % RING, 1)].squeeze(1).bitcast(F32),
                                 split_w[bass.ds(e + RING - 1, 1)].squeeze(0)).then_inc(s_w, 16)
                with sp.Else():
                    pass

            for j in range(3):
                load_tile(j, j)

            LATER = 2 * (RING - EARLY) - 2

            def step_b(j, u, r, in_b):
                ahead = 3
                if kind(j, in_b, ahead) == "list":
                    load_tile(j + ahead, (u + ahead) % 8)
                if isinstance(j, int) and j % 2 == 0 and j // 2 < RING - EARLY:
                    e = EARLY + j // 2
                    sp.wait_ge(s_w, 16 * e)
                    sp.dma_start(ring[:, e].bitcast(F32), split_w[e]).then_inc(s_w, 16)
                if kind(j, in_b, 0) == "list" and not (isinstance(j, int) and j <= LATER):
                    next_expert(j - LATER)
                if kind(j, in_b, 0) == "shared":
                    if isinstance(j, int) and j == SLOTS:
                        for i in range(4):
                            sp.wait_ge(s_ys[i], 16 * (SLOTS // 4))
                    wait(sp, s_fin, 2 * (j - SLOTS - 3) - 1)
                    sp.dma_start(yr[:, u % 4], routed_t[bass.ds(j - SLOTS, 1)].squeeze(0)).then_inc(s_yl[u % 4], 16)
                if kind(j, in_b, -4) == "shared":
                    sp.wait_ge(s_fin, 2 * (j - SLOTS - 3))
                    sp.dma_start(out[bass.ds(j - SLOTS - 4, 1)].squeeze(0),
                                 X1[:, bass.ds(j - SLOTS - 4, 1)].squeeze(1)).then_inc(s_store, 16)

            each_tile(sp, step_b)
            for t in range(TILES + DRAIN - 4, TILES):
                sp.wait_ge(s_fin, 2 * t + 2)
                sp.dma_start(out[t], X1[:, t]).then_inc(s_store, 16)
            sp.wait_ge(s_store, 16 * TILES)

        @block.gpsimd
        def _(pool):
            def load_x(c, p, r):
                wait(pool, s_x[p], 16 * r)
                pool.dma_start(X1[:, bass.ds(4 * c, 4), :], xg[bass.ds(c, 1)].squeeze(0)).then_inc(s_x[p], 16)

            for c in range(2):
                load_x(c, c, 0)
            with pool.Fori(1, GROUPS // 2) as i:
                for p in range(2):
                    load_x(2 * i + p, p, i)

            def scatter(a, p, r):
                wait_alone(pool, s_pos[3], a + 1)
                for j in range(GS):
                    for k in range(TOP):
                        i = TOP * j + k
                        nc.gpsimd.indirect_dma_start(
                            out=lists, out_offset=bass.IndirectOffsetOnAxis(ap=pos[p][:, i:i + 1], axis=0),
                            in_=x2[p][:, j, :], in_offset=None).then_inc(s_scat[p], 16)

            def add_h(b, p, r):
                pool.wait_ge(s_hsb, b + 1)
                xh = X1[:, bass.ds(4 * b, GS), O:D]
                nc.gpsimd.tensor_tensor(xh, xh, hsb[:, p, :, 0:O], ALU.add).then_inc(s_xh1, 1)

            stages(pool, (2, add_h), (0, scatter))

            def take_dest(j, u, r):
                wait_alone(pool, s_xl[u % 4], 16 * r + 16)
                wait(pool, s_ys[u % 4], 16 * (r - 1))
                e = pool.value_load(table[0:1, 0, bass.ds(j, 1)], min_val=0, max_val=E - 1)
                nc.gpsimd.tensor_copy(dest[u][:], xs[u % 4][:, bass.ds(e + TAG, 1)])
                nc.gpsimd.tensor_copy(gate_j[u][:], xs[u % 4][:, bass.ds(e + GATE, 1)]).then_inc(s_dest, 1)

            def scatter_y(j, u):
                wait_alone(pool, s_y, j + 1)
                pool.wait_ge(s_dest, j + 1)
                nc.gpsimd.indirect_dma_start(
                    out=routed, out_offset=bass.IndirectOffsetOnAxis(ap=dest[u][:, 0:1], axis=0),
                    in_=ysb[u % 4][:], in_offset=None, bounds_check=TOKENS * TOP - 1,
                    oob_is_err=False).then_inc(s_ys[u % 4], 16)

            def add_routed(t, u, r0):
                pool.wait_ge(s_yl[u % 4], 16 * r0 + 16)
                for k in range(1, TOP):
                    if k > 1:
                        pool.wait_ge(s_acc, (TOP - 1) * t + k - 1)
                    nc.gpsimd.tensor_tensor(yr[:, u % 4, 0:D], yr[:, u % 4, 0:D], yr[:, u % 4, k * D:(k + 1) * D],
                                            ALU.add).then_inc(s_acc, 1)

            pool.wait_ge(s_rows, 1)

            take_dest(0, 0, 0)
            take_dest(1, 1, 0)

            def step_b(j, u, r, in_b):
                if kind(j, in_b, -3) == "list":
                    scatter_y(j - 3, (u - 3) % 8)
                if kind(j, in_b, 2) == "list":
                    take_dest(j + 2, (u + 2) % 8, r + (u % 4 + 2) // 4)
                if kind(j, in_b, -3) == "shared":
                    add_routed(j - 3 - SLOTS, (u - 3) % 8, r + (u % 4 - 3) // 4 - SLOTS // 4)

            each_tile(pool, step_b)

        @block.scalar
        def _(act):
            nc.scalar.preload_act_table_set("natural_log_exp_and_others")
            act.wait_ge(s_const, 16 * CONSTS)

            def split_high(m, p, r):
                act.wait_ge(s_win, 16 * m + 16)
                if isinstance(m, int) and m == 0:
                    nc.scalar.activation(shared[:, 0], wst[:], ACT.Copy).then_inc(s_whi, 1)
                    return
                wait(act, s_wout[p], 16 * r)
                nc.scalar.activation(ring[:, p, 0], wst[:], ACT.Copy).then_inc(s_whi, 1)

            def guess(steps, variance, nw, g):
                act.wait_ge(variance, g + 1)
                nc.scalar.activation(nw[:, 1], nw[:, 0], ACT.Ln).then_inc(steps[0], 1)
                act.wait_ge(steps[0], g + 1)
                nc.scalar.activation(nw[:, 2], nw[:, 1], ACT.Exp, scale=-0.5).then_inc(steps[1], 1)

            def guess1(g, p, r):
                guess(s_ex1, s_ln1[2], nw1, g)

            def guess2(b, p, r):
                guess(s_ex2, s_x1[4], nw2, b)

            def exp_logits(a, p, r):
                act.wait_ge(s_lg, a + 1)
                wait(act, s_rt[0], a)
                nc.scalar.activation(ez[:].rearrange("p j e -> p (j e)"), p_lg, ACT.Exp, scale=-1.0).then_inc(s_ez, 1)

            def slope(b, p, r):
                act.wait_ge(s_nb, b + 1)
                nc.scalar.activation(att[:].rearrange("p j n -> p (j n)"), p_n[:], ACT.Copy,
                                     scale=SLOPE).then_inc(s_slope, 1)

            def exp_scores(b, p, r):
                act.wait_ge(s_att[2], b + 1)
                wait(act, s_tp, b)
                for j in range(GS):
                    last = nc.scalar.activation(prob[:, j], att[:, j], ACT.Exp, bias=nmax[:, j:j + 1],
                                                accum_out=psums[:, j:j + 1])
                last.then_inc(s_exp, 1)

            def norm1(c, p, r):
                act.wait_ge(s_ln1[6], c + 1)
                wait(act, s_t1, c - 1)
                for j in range(GS):
                    last = nc.scalar.activation(xn1[:, p, j], X1[:, bass.ds(4 * c + j, 1)].squeeze(1), ACT.Identity,
                                                bias=ln1[:, p, j, 1:2], scale=ln1[:, p, j, 0:1])
                last.then_inc(s_xn1, 1)

            def copy_probT(b, p, r):
                act.wait_ge(s_tp, b + 1)
                wait(act, s_out, b)
                nc.scalar.activation(probT[:].rearrange("p j e -> p (j e)"), p_pt[:], ACT.Copy).then_inc(s_pT, 1)

            def copy_xnT(c, p, r):
                act.wait_ge(s_t1, c + 1)
                wait(act, s_h, c)
                nc.scalar.activation(xnT[:, 0], p_t[0][:], ACT.Copy)
                nc.scalar.activation(xnT[:, 1], p_t[1][:], ACT.Copy).then_inc(s_xnT, 1)

            def copy_h(c, p, r):
                act.wait_ge(s_h, c + 1)
                wait(act, s_out, c - 1)
                wait(act, s_xh1, c - 1)
                for i in range(2):
                    last = nc.scalar.activation(hsb[:, p, 2 * i:2 * i + 2],
                                                p_h[i][:, 0:2 * (O + 2)].rearrange("p (j n) -> p j n", j=2), ACT.Copy)
                last.then_inc(s_hsb, 1)

            def norm2(b, p, r):
                act.wait_ge(s_x1[8], b + 1)
                wait(act, s_scat[p], 16 * GROUP_SCATTERS * r)
                for j in range(GS):
                    t = 4 * b + j
                    last = nc.scalar.activation(x2[p][:, j, 0:D], X1[:, bass.ds(t, 1)].squeeze(1), ACT.Identity,
                                                bias=ln2[:, bass.ds(t, 1), 1], scale=ln2[:, bass.ds(t, 1), 0])
                last.then_inc(s_x2, 1)

            def copy_x2T(b, p, r):
                act.wait_ge(s_t2, b + 1)
                wait(act, s_lg, b)
                nc.scalar.activation(x2T[:, 0], p_t[0][:], ACT.Copy)
                nc.scalar.activation(x2T[:, 1], p_t[1][:], ACT.Copy).then_inc(s_x2T, 1)

            def split_next(e, p, r):
                split_high(later(e, 1), p, r)

            def split_shared(c, p, r):
                if isinstance(c, int) and c == 0:
                    split_high(0, 0, 0)

            stages(act, (0, copy_x2T), (3, norm1), (0, exp_logits), (2, exp_scores), (3, copy_xnT), (1, guess2),
                   (3, split_next), (2, copy_probT), (4, guess1), (3, copy_h), (1, norm2), (4, split_shared),
                   (3, slope))

            act.wait_ge(s_rows, 1)
            for e in range(1, E, 2):
                pad_list(act, e, s_pad[1])

            def tile_high(j, u):
                act.wait_ge(s_tx, j + 1)
                nc.scalar.activation(xTh[:, u % 2].rearrange("p k t -> p (k t)"), p_xT[u % 2][:, 0:D],
                                     ACT.Copy).then_inc(s_xh, 1)

            def hidden_high(j, u):
                act.wait_ge(s_th, j + 1)
                nc.scalar.activation(hTh[:, u % 2].rearrange("p k t -> p (k t)"), p_hT[u % 2][:, 0:FF],
                                     ACT.Copy).then_inc(s_hh, 1)

            def silu(j, u):
                act.wait_ge(s_gu, j + 1)
                nc.scalar.activation(gate[:, u % 2], p_gu[u % 2][:, 0:FF], ACT.Silu).then_inc(s_sg, 1)

            def result(j, u, r):
                act.wait_ge(s_dn, j + 1)
                wait(act, s_ys[u % 4], 16 * r)
                act.wait_ge(s_dest, j + 1)
                nc.scalar.activation(ysb[u % 4][:], p_y[u % 2][:, 0:D], ACT.Copy,
                                     scale=gate_j[u][:, 0:1]).then_inc(s_y, 1)

            def norm_shared(j, u):
                t = j - SLOTS
                wait(act, s_tx, j - 3)
                if isinstance(j, int) and j < SLOTS + 4:
                    act.wait_ge(s_dest, j - 3)
                nc.scalar.activation(xs[u % 4][:, 0:D], X1[:, bass.ds(t, 1)].squeeze(1), ACT.Identity,
                                     bias=ln2[:, bass.ds(t, 1), 1], scale=ln2[:, bass.ds(t, 1), 0]).then_inc(s_xsh, 1)

            tile_high(0, 0)
            tile_high(1, 1)

            def step_b(j, u, r, in_b):
                if kind(j, in_b, -3) == "list":
                    result(j - 3, (u - 3) % 8, r + (u % 4 - 3) // 4)
                if kind(j, in_b, -1):
                    hidden_high(j - 1, (u - 1) % 8)
                if kind(j, in_b, 3) == "shared":
                    norm_shared(j + 3, (u + 3) % 8)
                if kind(j, in_b, 0):
                    silu(j, u)
                if kind(j, in_b, 2):
                    tile_high(j + 2, (u + 2) % 8)

            each_tile(act, step_b)

        @block.vector
        def _(dve):
            dve.wait_ge(s_const, 16 * CONSTS)
            nc.vector.tensor_copy(low_ones[:, 0:P], cs[:, C_LOW:C_LOW + P])
            nc.vector.memset(low_ones[:, P:2 * P], 1.0)
            nc.vector.memset(before[:, 0], 0.0)
            nc.vector.tensor_copy(tagbase[:], cs[:, C_TAG:C_TAG + GS])
            nc.vector.tensor_scalar(mask[:], adj_i[:], -1.0, 1.0, ALU.mult, ALU.add).then_inc(s_prep, 1)
            dve.wait_ge(s_prep, 1)
            nc.vector.tensor_scalar(mask[:], mask[:], NEG, None, ALU.mult).then_inc(s_prep, 1)
            dve.wait_ge(s_wa, 1)
            nc.vector.tensor_copy(wext[:, :, O:O + 2],
                                  p_h[0][:, 0:2 * KD].rearrange("p (k c) -> p k c", k=KD)).then_inc(s_prep, 1)

            def split_low(m, p):
                dve.wait_ge(s_whi, m + 1)
                first = isinstance(m, int) and m == 0
                dst = shared if first else ring[:, p]
                nc.vector.tensor_tensor(dst[:, 1], wst[:], dst[:, 0].bitcast(F32), ALU.subtract).then_inc(s_wlo, 1)


            def attention0(b, p, r):
                dve.wait_ge(s_slope, b + 1)
                nc.vector.tensor_tensor(att[:], att[:], p_n[:].rearrange("p (j n) -> p j n", j=GS),
                                        ALU.max).then_inc(s_att[0], 1)

            def attention1(b, p, r):
                dve.wait_ge(s_att[0], b + 1)
                nc.vector.tensor_tensor(att[:], att[:], mask[:].unsqueeze(1).to_broadcast([P, GS, P]),
                                        ALU.add).then_inc(s_att[1], 1)

            def attention2(b, p, r):
                dve.wait_ge(s_att[1], b + 1)
                nc.vector.tensor_reduce(nmax[:], att[:], AX_X, ALU.max, negate=True).then_inc(s_att[2], 1)

            def stats1_0(c, p, r):
                wait_alone(dve, s_x[p], 16 * r + 16)
                for j in range(GS):
                    last = nc.vector.bn_stats(st[:, j], X1[:, bass.ds(4 * c + j, 1)].squeeze(1))
                last.then_inc(s_ln1[0], 1)

            def stats1_1(c, p, r):
                wait_alone(dve, s_ln1[0], c + 1)
                for j in range(GS):
                    last = nc.vector.bn_aggr(mv[:, j], st[:, j])
                last.then_inc(s_ln1[1], 1)

            def stats1_2(c, p, r):
                dve.wait_ge(s_ln1[1], c + 1)
                nc.vector.tensor_scalar(nw1[:, 0], mv[:, :, 1], EPS, None, ALU.add).then_inc(s_ln1[2], 1)

            def newton(k, g, steps, first, nw, mean, scale, shift):
                if k > 0:
                    dve.wait_ge(steps[first + k - 1], g + 1)
                if k == 0:
                    ins = nc.vector.scalar_tensor_tensor(nw[:, 3], nw[:, 0], -0.5, nw[:, 2], ALU.mult, ALU.mult)
                elif k == 1:
                    ins = nc.vector.tensor_tensor(nw[:, 4], nw[:, 3], nw[:, 2], ALU.mult)
                elif k == 2:
                    ins = nc.vector.scalar_tensor_tensor(scale, nw[:, 4], 1.5, nw[:, 2], ALU.add, ALU.mult)
                else:
                    ins = nc.vector.scalar_tensor_tensor(shift, mean, -1.0, scale, ALU.mult, ALU.mult)
                ins.then_inc(steps[first + k], 1)

            def newton1(k):
                def part(c, p, r):
                    if k == 0:
                        dve.wait_ge(s_ex1[1], c + 1)
                        wait(dve, s_xn1, c - 1)
                    newton(k, c, s_ln1, 3, nw1, mv[:, :, 0], ln1[:, p, :, 0], ln1[:, p, :, 1])
                return part

            def newton2(k):
                def part(b, p, r):
                    if k == 0:
                        dve.wait_ge(s_ex2[1], b + 1)
                    newton(k, b, s_x1, 5, nw2, mv2[:, :, 0], ln2[:, bass.ds(4 * b, GS), 0],
                           ln2[:, bass.ds(4 * b, GS), 1])
                return part

            def add_graph0(b, p, r):
                dve.wait_ge(s_out, b + 1)
                nc.vector.reciprocal(rsum[:], psums[:]).then_inc(s_x1[0], 1)

            def add_graph1(b, p, r):
                dve.wait_ge(s_x1[0], b + 1)
                for j in range(GS):
                    xt = X1[:, bass.ds(4 * b + j, 1), 0:O].squeeze(1)
                    last = nc.vector.scalar_tensor_tensor(xt, p_o[:, j * O:(j + 1) * O], rsum[:, j:j + 1], xt,
                                                          ALU.mult, ALU.add)
                last.then_inc(s_x1[1], 1)

            def add_graph2(b, p, r):
                wait_alone(dve, s_xh1, b + 1)
                wait_alone(dve, s_x1[1], b + 1)
                for j in range(GS):
                    last = nc.vector.bn_stats(st2[:, j], X1[:, bass.ds(4 * b + j, 1)].squeeze(1))
                last.then_inc(s_x1[2], 1)

            def add_graph3(b, p, r):
                wait_alone(dve, s_x1[2], b + 1)
                for j in range(GS):
                    last = nc.vector.bn_aggr(mv2[:, j], st2[:, j])
                last.then_inc(s_x1[3], 1)

            def add_graph4(b, p, r):
                dve.wait_ge(s_x1[3], b + 1)
                nc.vector.tensor_scalar(nw2[:, 0], mv2[:, :, 1], EPS, None, ALU.add).then_inc(s_x1[4], 1)

            def route0(a, p, r):
                dve.wait_ge(s_ez, a + 1)
                nc.vector.tensor_scalar(aff1[:], ez[:], 1.0, None, ALU.add).then_inc(s_rt[0], 1)

            def route1(a, p, r):
                dve.wait_ge(s_rt[0], a + 1)
                nc.vector.reciprocal(aff[:], aff1[:]).then_inc(s_rt[1], 1)

            def route2(a, p, r):
                dve.wait_ge(s_rt[1], a + 1)
                nc.vector.tensor_tensor(score[:], aff[:], bias_s[:].unsqueeze(1).to_broadcast([P, GS, E]),
                                        ALU.add).then_inc(s_rt[2], 1)

            def route3(a, p, r):
                wait_alone(dve, s_rt[2], a + 1)
                for j in range(GS):
                    last = nc.vector.max(top8[:, j], score[:, j])
                last.then_inc(s_rt[3], 1)

            def route4(a, p, r):
                wait_alone(dve, s_rt[3], a + 1)
                for j in range(GS):
                    last = nc.vector.max_index(topi[:, j], top8[:, j], score[:, j])
                last.then_inc(s_rt[4], 1)

            def route5(a, p, r):
                dve.wait_ge(s_rt[4], a + 1)
                nc.vector.tensor_copy(topf[:], topi[:, :, 0:TOP]).then_inc(s_rt[5], 1)

            def route6(a, p, r):
                dve.wait_ge(s_rt[5], a + 1)
                iota = cs[:, C_IOTA:C_IOTA + E].unsqueeze(1).to_broadcast([P, TOP, E])
                for j in range(GS):
                    last = nc.vector.tensor_tensor(onehot[:, j], topf[:, j].unsqueeze(2).to_broadcast([P, TOP, E]),
                                                   iota, ALU.is_equal)
                last.then_inc(s_rt[6], 1)

            def route7(a, p, r):
                dve.wait_ge(s_rt[6], a + 1)
                with nc.allow_low_precision("zeros and ones"):
                    nc.vector.tensor_reduce(taken[:], onehot[:].rearrange("p j k e -> p j e k"), AX_X,
                                            ALU.add).then_inc(s_rt[7], 1)

            def route8(a, p, r):
                dve.wait_ge(s_rt[7], a + 1)
                nc.vector.tensor_tensor(sel[:], taken[:], aff[:], ALU.mult)
                nc.vector.tensor_reduce(newly[:], taken[:].rearrange("p j e -> p e j"), AX_X, ALU.add)
                nc.vector.scalar_tensor_tensor(tag1[:], onehot[:, :, 2], 2.0, taken[:], ALU.mult,
                                               ALU.add).then_inc(s_rt[8], 1)

            def route9(a, p, r):
                dve.wait_ge(s_rt[8], a + 1)
                nc.vector.tensor_tensor(tag2[:], tag1[:], onehot[:, :, 1], ALU.add)
                with nc.allow_low_precision("whole numbers up to 64"):
                    nc.vector.tensor_tensor(before[:, 1 - p], before[:, p], newly[:], ALU.add)
                nc.vector.tensor_reduce(den[:, 0], sel[:], AX_X, ALU.add).then_inc(s_rt[9], 1)

            def route10(a, p, r):
                dve.wait_ge(s_rt[9], a + 1)
                nc.vector.tensor_tensor(x2[p][:, :, TAG:GATE], tag2[:],
                                        tagbase[:].unsqueeze(2).to_broadcast([P, GS, E]), ALU.add)
                nc.vector.tensor_scalar(den[:, 1], den[:, 0], 1e-9, None, ALU.add).then_inc(s_rt[10], 1)

            def route11(a, p, r):
                dve.wait_ge(s_rt[10], a + 1)
                nc.vector.tensor_scalar(tagbase[:], tagbase[:], float(TOP * GS * P), None, ALU.add)
                nc.vector.reciprocal(den[:, 2], den[:, 1]).then_inc(s_rt[11], 1)

            def route12(a, p, r):
                dve.wait_ge(s_rt[11], a + 1)
                nc.vector.tensor_tensor(x2[p][:, :, GATE:ROW], aff[:], den[:, 2].unsqueeze(2).to_broadcast([P, GS, E]),
                                        ALU.mult).then_inc(s_rt[12], 1)

            def positions0(a, p, r):
                dve.wait_ge(s_rk, a + 1)
                nc.vector.tensor_tensor(rankb[:], p_rk.rearrange("p (j e) -> p j e", j=GS),
                                        cs[:, C_BASE:C_BASE + E].unsqueeze(1).to_broadcast([P, GS, E]),
                                        ALU.add).then_inc(s_pos[0], 1)

            def positions1(a, p, r):
                dve.wait_ge(s_pos[0], a + 1)
                for j in range(GS):
                    last = nc.vector.tensor_tensor(selpos[:, j], onehot[:, j],
                                                   rankb[:, j].unsqueeze(1).to_broadcast([P, TOP, E]), ALU.mult)
                last.then_inc(s_pos[1], 1)

            def positions2(a, p, r):
                dve.wait_ge(s_pos[1], a + 1)
                nc.vector.tensor_reduce(posf[:], selpos[:], AX_X, ALU.add).then_inc(s_pos[2], 1)

            def positions3(a, p, r):
                dve.wait_ge(s_pos[2], a + 1)
                nc.vector.tensor_copy(pos[p][:], posf[:].rearrange("p j k -> p (j k)")).then_inc(s_pos[3], 1)

            def split_next(e, p, r):
                split_low(later(e, 1), p)

            def split_shared(c, p, r):
                if isinstance(c, int) and c == 0:
                    split_low(0, 0)

            stages(dve, (1, add_graph0), (2, attention0), (3, newton1(0)), (2, attention1), (3, newton1(1)),
                   (1, add_graph1), (3, newton1(2)), (3, newton1(3)), (2, attention2), (1, add_graph2), (4, stats1_0),
                   (1, add_graph3), (0, route0), (4, stats1_1), (0, route1), (4, stats1_2), (0, route2),
                   (1, add_graph4), (0, route3), (0, route4), (0, route5), (0, route6), (1, newton2(0)), (0, route7),
                   (0, route8), (1, newton2(1)), (0, route9), (1, newton2(2)), (0, route10), (3, split_next),
                   (1, newton2(3)), (0, positions0), (4, split_shared), (0, route11), (0, positions1), (0, route12),
                   (0, positions2), (0, positions3))

            dve.wait_ge(s_cnt, 1)
            nc.vector.tensor_copy(cnt[:], bank[7][:, 0:E]).then_inc(s_tb, 1)
            dve.wait_ge(s_tb, 1)
            nc.vector.tensor_scalar(ntf[:], cnt[:], 1.0 / P, (P - 1) / 2 / P, ALU.mult, ALU.add).then_inc(s_tb, 1)
            nc.vector.tensor_copy(counts_i[:], cnt[0:1, :])
            dve.wait_ge(s_tb, 2)
            nc.vector.tensor_copy(nti[:], ntf[:]).then_inc(s_tb, 1)
            dve.wait_ge(s_tb, 3)
            nc.vector.tensor_scalar(ntf[:], nti[:], 1.0, None, ALU.max).then_inc(s_tb, 1)
            dve.wait_ge(s_tb, 4)
            nc.vector.tensor_tensor_scan(cum[:], cs[:, C_ONE:C_ONE + E], ntf[:], 0.0, ALU.mult, ALU.add)\
                .then_inc(s_tb, 1)
            dve.wait_ge(s_tb, 5)
            jt = cs[:, C_TILE:C_TILE + 2]
            nc.vector.tensor_tensor(ended[:], cum[:].unsqueeze(1).to_broadcast([P, 2, E]),
                                    jt.unsqueeze(2).to_broadcast([P, 2, E]), ALU.is_le).then_inc(s_tb, 1)
            dve.wait_ge(s_tb, 6)
            nc.vector.tensor_tensor(tmp3[:], ended[:], cs[:, C_MOVE:C_MOVE + E].unsqueeze(1).to_broadcast([P, 2, E]),
                                    ALU.mult)
            nc.vector.tensor_reduce(ej[:, 0], ended[:], AX_X, ALU.add)
            nc.vector.tensor_tensor(tmp2[:], ended[:], ntf[:].unsqueeze(1).to_broadcast([P, 2, E]),
                                    ALU.mult).then_inc(s_tb, 1)
            dve.wait_ge(s_tb, 7)
            nc.vector.tensor_reduce(tv[:, 3], tmp3[:], AX_X, ALU.add)
            nc.vector.tensor_reduce(ej[:, 1], tmp2[:], AX_X, ALU.add).then_inc(s_tb, 1)
            dve.wait_ge(s_tb, 8)
            nc.vector.tensor_tensor(ej[:, 2], jt, ej[:, 1], ALU.subtract)
            nc.vector.tensor_tensor(ej[:, 3], jt, ej[:, 1], ALU.is_equal)
            nc.vector.tensor_scalar(ej[:, 4], ej[:, 0], float(REGION), None, ALU.mult)
            nc.vector.tensor_scalar(ej[:, 6], ej[:, 0], float(E - RING), None, ALU.is_le)
            nc.vector.tensor_scalar(tv[:, 0], ej[:, 0], float(E - 1), None, ALU.min).then_inc(s_tb, 1)
            dve.wait_ge(s_tb, 9)
            nc.vector.scalar_tensor_tensor(ej[:, 5], ej[:, 2], float(P), ej[:, 4], ALU.mult, ALU.add)
            nc.vector.tensor_tensor(tv[:, 2], ej[:, 3], ej[:, 6], ALU.mult).then_inc(s_tb, 1)
            dve.wait_ge(s_tb, 10)
            nc.vector.tensor_scalar(tv[:, 1], ej[:, 5], float(E * REGION), None, ALU.min).then_inc(s_tb, 1)
            dve.wait_ge(s_tb, 12)
            nc.vector.tensor_copy(table[:, 0:2].rearrange("p v j -> p (v j)"), bank[6][0:1, :])
            nc.vector.tensor_copy(table[:, 2:4].rearrange("p v j -> p (v j)"), bank[5][0:1, :]).then_inc(s_rows, 1)

            def weights_in(j):
                e = dve.value_load(table[0:1, 0, bass.ds(j, 1)], min_val=0, max_val=E - 1)
                dve.wait_ge(s_w, 16 * (e + 1))

            def tile_low(j, u):
                dve.wait_ge(s_xh, j + 1)
                nc.vector.tensor_tensor(xTl[:, u % 2].rearrange("p k t -> p (k t)"), p_xT[u % 2][:, 0:D],
                                        xTh[:, u % 2].rearrange("p k t -> p (k t)").bitcast(F32),
                                        ALU.subtract).then_inc(s_xlo, 1)

            def hidden_low(j, u):
                dve.wait_ge(s_hh, j + 1)
                nc.vector.tensor_tensor(hTl[:, u % 2].rearrange("p k t -> p (k t)"), p_hT[u % 2][:, 0:FF],
                                        hTh[:, u % 2].rearrange("p k t -> p (k t)").bitcast(F32),
                                        ALU.subtract).then_inc(s_hl, 1)

            def multiply(j, u):
                dve.wait_ge(s_sg, j + 1)
                nc.vector.tensor_tensor(hid[:, u % 2], p_gu[u % 2][:, FF:WIDE], gate[:, u % 2],
                                        ALU.mult).then_inc(s_hid, 1)

            def finish(j, u):
                t = j - SLOTS
                xt = X1[:, bass.ds(t, 1)].squeeze(1)
                dve.wait_ge(s_acc, (TOP - 1) * (t + 1))
                dve.wait_ge(s_xsh, t + 1)
                nc.vector.tensor_tensor(xt, yr[:, u % 4, 0:D], xt, ALU.add).then_inc(s_fin, 1)
                dve.wait_ge(s_fin, 2 * t + 1)
                dve.wait_ge(s_dn, j + 1)
                nc.vector.tensor_tensor(xt, p_y[u % 2][:, 0:D], xt, ALU.add).then_inc(s_fin, 1)

            dve.wait_ge(s_rows, 1)
            weights_in(0)
            tile_low(0, 0)
            weights_in(1)
            tile_low(1, 1)

            def step_b(j, u, r, in_b):
                if kind(j, in_b, -3) == "shared":
                    finish(j - 3, (u - 3) % 8)
                if kind(j, in_b, -1):
                    hidden_low(j - 1, (u - 1) % 8)
                if kind(j, in_b, 0):
                    multiply(j, u)
                if kind(j, in_b, 2) == "list":
                    weights_in(j + 2)
                if kind(j, in_b, 2):
                    tile_low(j + 2, (u + 2) % 8)

            each_tile(dve, step_b)

        @block.tensor
        def _(pe):
            pe.wait_ge(s_const, 16 * CONSTS)
            for k in range(KD):
                last = nc.tensor.matmul(p_h[0][:, 2 * k:2 * k + 2], wts[:, k * P:(k + 1) * P], ats[:],
                                        start=True, stop=True)
            last.then_inc(s_wa, 1)
            pe.wait_ge(s_prep, 3)

            def score_sums(b, p, r):
                pe.wait_ge(s_hsb, b + 1)
                wait(pe, s_pT, b)
                for j in range(GS):
                    dst = p_n[:, j * P:(j + 1) * P]
                    nc.tensor.matmul(dst, hsb[:, p, j, O + 1:O + 2].to_broadcast([P, P]), ident, start=True, stop=False)
                    last = nc.tensor.matmul(dst, ident, hsb[:, p, j, O:O + 1].to_broadcast([P, P]),
                                            start=False, stop=True)
                last.then_inc(s_nb, 1)

            def transpose_prob(b, p, r):
                pe.wait_ge(s_exp, b + 1)
                for j in range(GS):
                    last = nc.tensor.transpose(p_pt[:, j * P:(j + 1) * P], prob[:, j], ident)
                last.then_inc(s_tp, 1)

            def transpose_xn1(c, p, r):
                pe.wait_ge(s_xn1, c + 1)
                wait(pe, s_x2T, c - 2)
                wait(pe, s_xnT, c)
                for k in range(KD):
                    for j in range(GS):
                        last = nc.tensor.transpose(p_t[k][:, j * P:(j + 1) * P], xn1[:, p, j, k * P:(k + 1) * P], ident)
                last.then_inc(s_t1, 1)

            def attend(b, p, r):
                pe.wait_ge(s_pT, b + 1)
                wait(pe, s_x1[1], b)
                for j in range(GS):
                    last = nc.tensor.matmul(p_o[:, j * O:(j + 1) * O], probT[:, j], hsb[:, p, j, 0:O],
                                            start=True, stop=True)
                last.then_inc(s_out, 1)

            def ranks(a, p, r):
                pe.wait_ge(s_rt[7], a + 1)
                nc.tensor.matmul(p_rk, lower, taken[:].rearrange("p j e -> p (j e)"), start=True, stop=False)
                for j in range(GS - 1):
                    n = GS - 1 - j
                    nc.tensor.matmul(p_rk[:, (j + 1) * E:].rearrange("p (j e) -> p j e", j=n), ones,
                                     taken[:, j:j + 1].to_broadcast([P, n, E]), start=False, stop=False)
                nc.tensor.matmul(p_rk.rearrange("p (j e) -> p j e", j=GS), ones,
                                 before[:, p:p + 1].to_broadcast([P, GS, E]), start=False, stop=True).then_inc(s_rk, 1)

            def project(c, p, r):
                pe.wait_ge(s_xnT, c + 1)
                wait(pe, s_hsb, c)
                for j in range(GS):
                    for k in range(KD):
                        last = nc.tensor.matmul(p_h[j // 2][:, (j % 2) * (O + 2):(j % 2 + 1) * (O + 2)],
                                                xnT[:, k, j * P:(j + 1) * P], wext[:, k],
                                                start=(k == 0), stop=(k == KD - 1))
                last.then_inc(s_h, 1)

            def transpose_x2(b, p, r):
                pe.wait_ge(s_x2, b + 1)
                for k in range(KD):
                    for j in range(GS):
                        last = nc.tensor.transpose(p_t[k][:, j * P:(j + 1) * P], x2[p][:, j, k * P:(k + 1) * P], ident)
                last.then_inc(s_t2, 1)

            def logits(b, p, r):
                pe.wait_ge(s_x2T, b + 1)
                wait(pe, s_ez, b)
                for j in range(GS):
                    for k in range(KD):
                        last = nc.tensor.matmul(p_lg[:, j * E:(j + 1) * E], x2T[:, k, j * P:(j + 1) * P], gws[:, k],
                                                start=(k == 0), stop=(k == KD - 1))
                last.then_inc(s_lg, 1)

            stages(pe, (0, transpose_x2), (0, logits), (3, transpose_xn1), (2, transpose_prob), (3, project),
                   (2, attend), (0, ranks), (3, score_sums))

            pe.wait_ge(s_rt[12], GROUPS)
            pe.wait_ge(s_pos[3], GROUPS)
            nc.tensor.matmul(bank[7][:, 0:E], ones, before[:, GROUPS % 2], start=True, stop=True).then_inc(s_cnt, 1)
            pe.wait_ge(s_tb, 11)
            for v in range(4):
                for h in range(2):
                    at0 = (v % 2) * 2 * P + h * P
                    last = nc.tensor.transpose(bank[6 - v // 2][0:1, at0:at0 + P], tv[:, v, h:h + 1], ident)
            last.then_inc(s_tb, 1)
            pe.wait_ge(s_rows, 1)

            def transpose_tile(j, u, r, what):
                if what == "list":
                    pe.wait_ge(s_xl[u % 4], 16 * r + 16)
                else:
                    pe.wait_ge(s_xsh, j - SLOTS + 1)
                for k in range(KD):
                    last = nc.tensor.transpose(p_xT[u % 2][:, k * P:(k + 1) * P],
                                               xs[u % 4][:, k * P:(k + 1) * P], ident)
                last.then_inc(s_tx, 1)

            ring_w = ring[:].rearrange("p r h c -> p (r h c)")
            places = [pe.alloc_register(f"place{i}") for i in range(4)]

            def load_place(j, u):
                pe.reg_load(places[u % 4], table[0:1, 3, bass.ds(j, 1)])

            def product(dst, xh, xl, u, what, at0, width, first, last_one):
                if what == "shared":
                    wh, wl = (shared[:, h, at0:at0 + width] for h in range(2))
                else:
                    place = pe.snap(places[u % 4], min_val=0, max_val=(RING - 1) * 2 * WX)
                    wh, wl = (ring_w[:, bass.ds(place + (h * WX + at0), width)] for h in range(2))
                nc.tensor.matmul(dst, xh, wh, start=first, stop=False)
                nc.tensor.matmul(dst, xl, wh, start=False, stop=False)
                return nc.tensor.matmul(dst, xh, wl, start=False, stop=last_one)

            def gate_up(j, u, what, k):
                if k == 0:
                    pe.wait_ge(s_xlo, j + 1)
                last = product(p_gu[u % 2][:, 0:WIDE], xTh[:, u % 2, k], xTl[:, u % 2, k], u, what, k * WIDE, WIDE,
                               k == 0, k == KD - 1)
                if k == KD - 1:
                    last.then_inc(s_gu, 1)

            def transpose_hidden(j, u):
                pe.wait_ge(s_hid, j + 1)
                for k in range(KF):
                    last = nc.tensor.transpose(p_hT[u % 2][:, k * P:(k + 1) * P],
                                               hid[:, u % 2, k * P:(k + 1) * P], ident)
                last.then_inc(s_th, 1)

            def down(j, u, what):
                pe.wait_ge(s_hl, j + 1)
                for k in range(KF):
                    last = product(p_y[u % 2][:, 0:D], hTh[:, u % 2, k], hTl[:, u % 2, k], u, what,
                                   KD * WIDE + k * D, D, k == 0, k == KF - 1)
                last.then_inc(s_dn, 1)

            load_place(0, 0)
            transpose_tile(0, 0, 0, "list")
            transpose_tile(1, 1, 0, "list")

            def step_b(j, u, r, in_b):
                what = kind(j, in_b, 0)
                if what:
                    gate_up(j, u, what, 0)
                    gate_up(j, u, what, 1)
                if kind(j, in_b, -1):
                    transpose_hidden(j - 1, (u - 1) % 8)
                if kind(j, in_b, -2):
                    down(j - 2, (u - 2) % 8, kind(j, in_b, -2))
                if kind(j, in_b, 2):
                    transpose_tile(j + 2, (u + 2) % 8, r + (u % 4 + 2) // 4, kind(j, in_b, 2))
                if kind(j, in_b, 1) == "list":
                    load_place(j + 1, (u + 1) % 8)

            each_tile(pe, step_b)


def kernel(x, adj, L0_gnn_W, L0_gnn_a, L0_ffn_gate_w, L0_ffn_expert_bias, L0_ffn_shared_gate_up,
           L0_ffn_shared_down, L0_ffn_expert_gate_up, L0_ffn_expert_down):
    import numpy as np
    import concourse.bacc as bacc
    from concourse.bass_utils import run_bass_kernel_spmd

    def chunks(a):
        n, kp, m = a.shape
        return a.reshape(n, kp // P, P, m).transpose(0, 2, 1, 3).reshape(n, P, -1)

    gate_up = np.concatenate([np.asarray(L0_ffn_shared_gate_up)[None], np.asarray(L0_ffn_expert_gate_up)])
    down = np.concatenate([np.asarray(L0_ffn_shared_down)[None], np.asarray(L0_ffn_expert_down)])
    weights = np.concatenate([chunks(gate_up.transpose(0, 2, 1)), chunks(down.transpose(0, 2, 1))], axis=2)
    w = np.asarray(L0_gnn_W)
    arrays = {
        "x": np.asarray(x),
        "adj": np.asarray(adj),
        "w": chunks(w[None])[0].reshape(P, KD, O),
        "wt": w.T,
        "at": np.asarray(L0_gnn_a)[:, :, 0].T,
        "gate_wt": chunks(np.asarray(L0_ffn_gate_w).T[None])[0].reshape(P, KD, E),
        "bias": np.broadcast_to(np.asarray(L0_ffn_expert_bias), (P, E)),
        "weights": weights,
        "consts": constants(),
    }
    arrays = {f"in_{k}": np.ascontiguousarray(v) for k, v in arrays.items()}
    nc = bacc.Bacc("TRN2", target_bir_lowering=False, num_devices=1)
    aps = [nc.dram_tensor(k, v.shape, mybir.dt.from_np(v.dtype), kind="ExternalInput").ap() for k, v in arrays.items()]
    out = nc.dram_tensor("out_0", (TILES, P, D), F32, kind="ExternalOutput").ap()
    build(nc, *aps, out)
    r = run_bass_kernel_spmd(nc, [arrays], core_ids=[0])
    return r.results[0]["out_0"]
```
